# Optimizing a Trainium2 kernel written in Bass

```python
import numpy as np
import jax
import jax.numpy as jnp

def _softmax(x, axis=-1):
    return jax.nn.softmax(x, axis=axis)

def _gelu(x):
    return jax.nn.gelu(x, approximate=True)

def _silu(x):
    return jax.nn.silu(x)

def _sigmoid(x):
    return jax.nn.sigmoid(x)

def _layernorm(x, axis=-1, eps=1e-05):
    m = jnp.mean(x, axis=axis, keepdims=True)
    v = jnp.var(x, axis=axis, keepdims=True)
    return (x - m) / jnp.sqrt(v + eps)

def _scatter_add(tgt, idx, src, axis=0):
    return tgt.at[idx].add(src)

def _segment_sum(src, seg, n):
    return jax.ops.segment_sum(src, seg, n)
kernel_name = 'mk_flamingo_gated_d1_seqx_r8_086304'

def setup_inputs(seed: int=0):
    np.random.seed(seed)
    _w = jnp.asarray

    def _rec_inputs():
        import jax
        import jax.numpy as jnp
        _rk = jax.random.key(seed)
        x = -0.0002928 + 1 * jax.random.normal(jax.random.fold_in(_rk, 1), (32, 64, 128), jnp.float32)
        _lenS = 64 - jax.random.randint(jax.random.fold_in(_rk, 7), (32,), 0, max(1, 64 // 4) + 1, jnp.int32)
        _lenS2 = 64 - jax.random.randint(jax.random.fold_in(_rk, 8), (32,), 0, max(1, 64 // 4) + 1, jnp.int32)
        _ctx_1024P = jax.random.normal(jax.random.fold_in(_rk, 11), (32, 16, 128), jnp.float32)
        _ctx_1024c = jax.random.dirichlet(jax.random.fold_in(_rk, 511), 0.3 * jnp.ones((16,), jnp.float32), (32, 64))
        _ctx_1024t = jnp.einsum('bsk,bkd->bsd', _ctx_1024c, _ctx_1024P)
        _ctx_1024t = _ctx_1024t * jax.lax.rsqrt(jnp.mean(jnp.square(_ctx_1024t)) + 1e-12) * 0.953939
        ctx_1024 = -1.39393e-06 + 0.999914 * (_ctx_1024t + 0.3 * jax.random.normal(jax.random.fold_in(_rk, 611), (32, 64, 128), jnp.float32))
        _g = jax.random.normal(jax.random.fold_in(_rk, 9001), (2, 1), jnp.float32)
        _g = jnp.sign(_g) * jnp.maximum(jnp.abs(_g), 1.0) + (_g == 0) * 1.0
        g_xattn = _g[0]
        g_ffn = _g[1]
        return (x, ctx_1024, g_xattn, g_ffn)
    x, ctx_1024, g_xattn, g_ffn = _rec_inputs()

    def _L0_xattn_setup():
        import jax, jax.numpy as jnp
        import numpy as np
        EMBED_DIM = 128
        NUM_HEADS = 16
        HEAD_DIM = EMBED_DIM // NUM_HEADS
        key = jax.random.key(seed)
        ks = jax.random.split(key, 11)
        B, S, D = (2, 256, EMBED_DIM)
        scale = 1.0 / np.sqrt(D)
        inp = {'query': jax.random.normal(ks[0], (B, S, D), jnp.float32), 'key': jax.random.normal(ks[1], (B, S, D), jnp.float32), 'value': jax.random.normal(ks[2], (B, S, D), jnp.float32), 'Wq': jax.random.normal(ks[3], (D, D), jnp.float32) * scale, 'bq': jnp.zeros((D,), jnp.float32), 'Wk': jax.random.normal(ks[4], (D, D), jnp.float32) * scale, 'bk': jnp.zeros((D,), jnp.float32), 'Wv': jax.random.normal(ks[5], (D, D), jnp.float32) * scale, 'bv': jnp.zeros((D,), jnp.float32), 'Wo': jax.random.normal(ks[6], (D, D), jnp.float32) * scale, 'bo': jnp.zeros((D,), jnp.float32)}
        return inp
    _L0_xattn_all = _L0_xattn_setup()
    _L0_xattn_in = {k: v for k, v in _L0_xattn_all.items() if k in ('Wq', 'bq', 'Wk', 'bk', 'Wv', 'bv', 'Wo', 'bo')}
    del _L0_xattn_all

    def _L0_ffn_setup():
        import jax, jax.numpy as jnp
        import numpy as np
        EPS = 1e-05
        HEADS = 8
        DIM_KEY = 128
        K = 16
        NUM_KEYS = 32
        key = jax.random.key(seed)
        ks = jax.random.split(key, 5)
        B, T, D = (1, 128, 128)
        x = jax.random.normal(ks[0], (B, T, D), dtype=jnp.float32)
        norm_w = jnp.ones((D,), dtype=jnp.float32)
        wq = jax.random.normal(ks[1], (D, DIM_KEY * HEADS * 2), dtype=jnp.float32) * 0.02
        keys = jax.random.normal(ks[2], (HEADS, NUM_KEYS, 2, DIM_KEY), dtype=jnp.float32) * 0.02
        expert_down = jax.random.normal(ks[3], (NUM_KEYS * NUM_KEYS, D), dtype=jnp.float32) * 0.02
        expert_up = jax.random.normal(ks[4], (NUM_KEYS * NUM_KEYS, D), dtype=jnp.float32) * 0.02
        return {'x': x, 'norm_w': norm_w, 'wq': wq, 'keys': keys, 'expert_down': expert_down, 'expert_up': expert_up}
    _L0_ffn_all = _L0_ffn_setup()
    _L0_ffn_in = {k: v for k, v in _L0_ffn_all.items() if k in ('norm_w', 'wq', 'keys', 'expert_down', 'expert_up')}
    del _L0_ffn_all
    return {'x': x, 'ctx_1024': ctx_1024, 'g_xattn': g_xattn, 'g_ffn': g_ffn, 'L0_xattn_Wq': _L0_xattn_in['Wq'], 'L0_xattn_bq': _L0_xattn_in['bq'], 'L0_xattn_Wk': _L0_xattn_in['Wk'], 'L0_xattn_bk': _L0_xattn_in['bk'], 'L0_xattn_Wv': _L0_xattn_in['Wv'], 'L0_xattn_bv': _L0_xattn_in['bv'], 'L0_xattn_Wo': _L0_xattn_in['Wo'], 'L0_xattn_bo': _L0_xattn_in['bo'], 'L0_ffn_norm_w': _L0_ffn_in['norm_w'], 'L0_ffn_wq': _L0_ffn_in['wq'], 'L0_ffn_keys': _L0_ffn_in['keys'], 'L0_ffn_expert_down': _L0_ffn_in['expert_down'], 'L0_ffn_expert_up': _L0_ffn_in['expert_up']}

def reference(x, ctx_1024, g_xattn, g_ffn, L0_xattn_Wq, L0_xattn_bq, L0_xattn_Wk, L0_xattn_bk, L0_xattn_Wv, L0_xattn_bv, L0_xattn_Wo, L0_xattn_bo, L0_ffn_norm_w, L0_ffn_wq, L0_ffn_keys, L0_ffn_expert_down, L0_ffn_expert_up):
    import jax
    import jax.numpy as jnp

    def _L0_xattn_ref(query, key, value, Wq, bq, Wk, bk, Wv, bv, Wo, bo):
        import jax, jax.numpy as jnp
        import numpy as np
        EMBED_DIM = 128
        NUM_HEADS = 16
        HEAD_DIM = EMBED_DIM // NUM_HEADS
        B, S, D = query.shape
        H, Hd = (NUM_HEADS, HEAD_DIM)

        def split_heads(x):
            return x.reshape(B, S, H, Hd).transpose(0, 2, 1, 3)
        Q = split_heads(query @ Wq.T + bq)
        K = split_heads(key @ Wk.T + bk)
        V = split_heads(value @ Wv.T + bv)
        scores = jnp.einsum('bhqd,bhkd->bhqk', Q, K) / np.sqrt(Hd).astype(jnp.float32)
        attn = jax.nn.softmax(scores, axis=-1)
        out = jnp.einsum('bhqk,bhkd->bhqd', attn, V)
        out = out.transpose(0, 2, 1, 3).reshape(B, S, D)
        return out @ Wo.T + bo

    def _L0_ffn_ref(x, norm_w, wq, keys, expert_down, expert_up):
        import jax, jax.numpy as jnp
        import numpy as np
        EPS = 1e-05
        HEADS = 8
        DIM_KEY = 128
        K = 16
        NUM_KEYS = 32
        B, T, D = x.shape
        inv = jax.lax.rsqrt(jnp.mean(x * x, axis=-1, keepdims=True) + EPS)
        x_norm = x * inv * norm_w
        q = (x_norm @ wq).reshape(B, T, HEADS, 2, DIM_KEY)
        sim = jnp.einsum('bthpd,hkpd->pbthk', q, keys)
        s1, i1 = jax.lax.top_k(sim[0], K)
        s2, i2 = jax.lax.top_k(sim[1], K)
        all_idx = (i1[..., :, None] * NUM_KEYS + i2[..., None, :]).reshape(B, T, HEADS, K * K)
        all_scores = (s1[..., :, None] + s2[..., None, :]).reshape(B, T, HEADS, K * K)
        final_scores, pk = jax.lax.top_k(all_scores, K)
        final_idx = jnp.take_along_axis(all_idx, pk, axis=-1)
        wd = expert_down[final_idx]
        wu = expert_up[final_idx]
        hidden = jnp.einsum('btd,bthkd->bthk', x_norm, wd)
        hidden = jax.nn.gelu(hidden, approximate=False)
        hidden = hidden * jax.nn.relu(final_scores)
        out = jnp.einsum('bthk,bthkd->btd', hidden, wu)
        return out
    x = x + jnp.tanh(g_xattn[0]) * _L0_xattn_ref(_layernorm(x, axis=-1), ctx_1024, ctx_1024, L0_xattn_Wq, L0_xattn_bq, L0_xattn_Wk, L0_xattn_bk, L0_xattn_Wv, L0_xattn_bv, L0_xattn_Wo, L0_xattn_bo)
    x = x + jnp.tanh(g_ffn[0]) * _L0_ffn_ref(_layernorm(x, axis=-1), L0_ffn_norm_w, L0_ffn_wq, L0_ffn_keys, L0_ffn_expert_down, L0_ffn_expert_up)
    return x

_drawn_inputs = setup_inputs


def setup_inputs(seed=0):
    import zlib

    import numpy as np

    out = dict(_drawn_inputs(seed))
    spreads = {'L0_xattn_bq': (0.0, 0.439),
     'L0_xattn_bk': (0.0, 0.8),
     'L0_xattn_bv': (0.0, 0.1),
     'L0_xattn_bo': (0.0, 0.1),
     'L0_ffn_norm_w': (1.0, 0.6)}
    factors = {'L0_ffn_wq': 8.0, 'L0_ffn_keys': 8.0, 'L0_ffn_expert_down': 8.0, 'L0_ffn_expert_up': 8.0}
    for name, (base, spread) in spreads.items():
        noise = np.random.default_rng([zlib.crc32(name.encode()), seed]).standard_normal(out[name].shape)
        drawn = base * np.exp(spread * noise) if base else spread * noise
        out[name] = jnp.asarray(drawn.astype(out[name].dtype))
    for name, factor in factors.items():
        out[name] = (out[name] * factor).astype(out[name].dtype)
    return out
```

```python
from contextlib import ExitStack

import concourse.bass as bass
from concourse import mybir

ALU = mybir.AluOpType
ACT = mybir.ActivationFunctionType
AX = mybir.AxisListType
F32 = mybir.dt.float32
F32R = mybir.dt.float32r

P = 128
B, S = 32, 64
D = 128
T = B * S
TILES = T // P
PAIR = P // S
H = 16
HD = D // H
G = 2
HG = H // G
HP = H // 2
VW = HD + 1
FH = 8
K = 16
NK = 32
SIDES = 2
LISTS = FH * SIDES
E = NK * NK
EC = E // P
REACH = [K // (a + 1) for a in range(K)]
CAND = sum(REACH)
LOWEST = -3.0e38
BELOW = 1.0 - 2.0 ** -21
EPS = 1e-5
SCALE = float(HD) ** -0.5


def flamingo_kernel(nc, x, ctx_in, g_attn, g_ffn, wq, bq, wk, bk, wv, bv, wo, bo,
                    norm_w, wq_ffn, keys, down, up, ident_in, head_mask_in, value_mask_in, select_in, out):
    x_view = x.rearrange("(t two) s d -> (two s) t d", two=PAIR)
    ctx_view = ctx_in.rearrange("(t two) s d -> t (two s) d", two=PAIR)
    out_view = out.rearrange("(t two) s d -> (two s) t d", two=PAIR)

    with ExitStack() as stack:
        def sb(name, shape, dt=F32):
            return stack.enter_context(nc.sbuf_tensor(name, shape, dt))

        def ps(name, shape, dt=F32):
            return stack.enter_context(nc.psum_tensor(name, shape, dt))

        def sem(name):
            return stack.enter_context(nc.semaphore(name))

        ident = sb("ident", [P, P])
        head_mask = sb("head_mask", [P, HG])
        value_mask = sb("value_mask", [P, H])
        weights = sb("weights", [P, 4, D])
        weights_t = sb("weights_t", [P, 4, D])
        bias_rows = sb("bias_rows", [4, D])
        bias_cols = sb("bias_cols", [P, 4])
        gate_in = sb("gate_in", [P, 2])
        gate = sb("gate", [P, 2])
        bo_rows = sb("bo_rows", [P, D])
        minus_half = sb("minus_half", [P, TILES])

        x_all = sb("x_all", [P, TILES, D])
        x_biased = sb("x_biased", [P, TILES, D])
        x2_all = sb("x2_all", [P, TILES, D])
        stats = sb("stats", [P, TILES, 6])
        mean_var = sb("mean_var", [P, TILES, 2])
        rstd = sb("rstd", [P, TILES])

        ctx_sb = [sb(f"ctx_sb{b}", [P, D]) for b in range(2)]
        xn = [sb(f"xn{b}", [P, D]) for b in range(2)]
        x_t = [sb(f"x_t{b}", [P, P]) for b in range(2)]
        ctx_t = [sb(f"ctx_t{b}", [P, PAIR, 2, S]) for b in range(2)]
        q_t = [sb(f"q_t{b}", [P, P]) for b in range(2)]
        k_t = [sb(f"k_t{b}", [P, P]) for b in range(2)]
        k_masked = [sb(f"k_masked{b}", [P, PAIR, HG, S]) for b in range(2)]
        v_blocks = [sb(f"v_blocks{b}", [P, PAIR, H, VW]) for b in range(2)]
        row_max = sb("row_max", [P, H])
        shifted = [sb(f"shifted{b}", [P, H * S]) for b in range(2)]
        probs = [sb(f"probs{b}", [P, H * S]) for b in range(2)]
        probs_t = [sb(f"probs_t{b}", [P, HP, P]) for b in range(2)]
        row_rec = sb("row_rec", [P, H])
        mixed_sb = [sb(f"mixed_sb{b}", [P, D]) for b in range(2)]
        mixed_t = [sb(f"mixed_t{b}", [P, P]) for b in range(2)]

        banks = ps("banks", [P, 8, 512])
        ps_turned, ps_qk, ps_v = (banks[:, n, :].rearrange("p (n c) -> p n c", n=4) for n in range(3))
        ps_out = banks[:, 3, :]
        scores_ps = banks[:, 4:6, :]
        probs_t_ps = banks[:, 6:8, :].rearrange("p n (m c) -> p (n m) c", c=P)
        ring = [banks[:, 2 * n:2 * n + 2, :].rearrange("p n c -> p (n c)") for n in range(3)]
        mix_w_ps = banks[:, 6:8, :].rearrange("p n c -> p (n c)")
        x_t_ps, ctx_t_ps, mix_t_ps = (ps_turned[:, n, :] for n in range(3))
        mix_ps = ps_out[:, 0:H * VW]
        y_ps = ps_out[:, 256:256 + D]

        select = sb("select", [P, E], F32R)
        norm_col = sb("norm_col", [P, 1])
        stage = sb("stage", [P, LISTS, P])
        keys_sb = sb("keys_sb", [P, FH * NK // P, SIDES, P])
        down_sb = sb("down_sb", [P, EC, D])
        up_sb = sb("up_sb", [P, EC, D])
        keys_t = sb("keys_t", [P, 2 * SIDES, P])
        wq_t = sb("wq_t", [P, LISTS, P])
        key_w = sb("key_w", [P, LISTS * NK])
        down_t = sb("down_t", [P, EC, P])

        fn = [sb(f"fn{b}", [P, D]) for b in range(2)]
        fn_t = [sb(f"fn_t{b}", [P, P]) for b in range(2)]
        sims = [sb(f"sims{b}", [P, LISTS, NK]) for b in range(2)]
        parts = [sb(f"parts{b}", [P, FH, SIDES, 2, NK]) for b in range(2)]
        parts_t = [sb(f"parts_t{b}", [P, FH, P], F32R) for b in range(2)]
        struck = sb("struck", [P, LISTS, NK])
        top = sb("top", [P, LISTS, K])
        cand = sb("cand", [P, FH, CAND])
        cand_struck = sb("cand_struck", [P, FH, CAND])
        best = sb("best", [P, FH, K])
        least = [sb(f"least{b}", [P, FH]) for b in range(2)]
        least_neg = [sb(f"least_neg{b}", [P, FH]) for b in range(2)]
        DEEP = 4
        excess = [sb(f"excess{n}", [P, E]) for n in range(DEEP)]
        base = [sb(f"base{n}", [P, E]) for n in range(DEEP)]
        hidden = [sb(f"hidden{b}", [P, EC * P]) for b in range(2)]
        mix_y = sb("mix_y", [P, EC, P])
        ffn_y = [sb(f"ffn_y{b}", [P, D]) for b in range(2)]
        result = [sb(f"result{b}", [P, D]) for b in range(2)]

        ffn_loaded = sem("ffn_loaded")
        sel_loaded = sem("sel_loaded")
        filled = sem("filled")
        copied = sem("copied")
        setup_ready = sem("setup_ready")
        ffn_stats = sem("ffn_stats")
        ffn_rstd = sem("ffn_rstd")
        fn_ready = sem("fn_ready")
        parts_ready = sem("parts_ready")
        ranked = sem("ranked")
        least_step = sem("least_step")
        least_ready = sem("least_ready")
        base_ready = sem("base_ready")
        head_summed = sem("head_summed")
        y_ready = sem("y_ready")
        added = sem("added")

        KEYS_JOB, WQ_JOB, DOWN_JOB, KEY_W_JOB = 0, 1, 3, 4
        FIRST = 11
        BODY = ("S0", "S1", "S2", "hid", "x", "S3", "sim", "S4", "S5", "split", "S6", "S7")
        ABSENT = {TILES - 2: ("sim",), TILES - 1: ("hid", "sim", "split")}

        def job(t, kind):
            at = BODY.index(kind)
            if not isinstance(t, int):
                return t * len(BODY) + (FIRST + at)
            missing = sum(len(kinds) for body, kinds in ABSENT.items() if body < t)
            missing += sum(BODY.index(kind) < at for kind in ABSENT.get(t, ()))
            return FIRST + t * len(BODY) + at - missing

        def slot(t, kind):
            return (job(t, kind) if isinstance(t, int) else FIRST + BODY.index(kind)) % 3

        LAST_JOB = job(TILES, "S0")

        def turn_job(tile):
            return (5, 7)[tile] if isinstance(tile, int) and tile < 2 else job(tile - 2, "x")

        def sims_job(tile):
            return (6, 8)[tile] if isinstance(tile, int) and tile < 2 else job(tile - 2, "sim")

        def hidden_job(tile):
            return 9 if isinstance(tile, int) and tile < 1 else job(tile - 1, "hid")

        def parts_job(tile):
            return 10 if isinstance(tile, int) and tile < 1 else job(tile - 1, "split")

        w_loaded = sem("w_loaded")
        x_loaded = sem("x_loaded")
        ctx_loaded = [sem(f"ctx_loaded{b}") for b in range(2)]
        w_transposed = sem("w_transposed")
        w_ready = sem("w_ready")
        gate_ready = sem("gate_ready")
        stats_step = sem("stats_step")
        rstd_ready = sem("rstd_ready")
        pool_step = sem("pool_step")
        xb_ready = sem("xb_ready")
        ones_ready = sem("ones_ready")
        xn_ready = sem("xn_ready")
        xc_transposed = sem("xc_transposed")
        xc_ready = sem("xc_ready")
        projected = sem("projected")
        qk_ready = sem("qk_ready")
        k_masked_ready = sem("k_masked_ready")
        v_ready = sem("v_ready")
        scored = sem("scored")
        max_ready = sem("max_ready")
        shift_done = sem("shift_done")
        exp_done = sem("exp_done")
        probs_transposed = sem("probs_transposed")
        probs_t_ready = sem("probs_t_ready")
        mixed = sem("mixed")
        rec_ready = sem("rec_ready")
        mixed_ready = sem("mixed_ready")
        mixed_transposed = sem("mixed_transposed")
        mixed_t_ready = sem("mixed_t_ready")
        attn_out = sem("attn_out")
        x2_ready = sem("x2_ready")
        stored = [sem(f"stored{b}") for b in range(2)]

        N_W = 4 + 1 + 1 + 2 + 3

        def attention_sweep(eng, step):
            step(0, 0, 0, False, True, True)
            step(1, 0, 1, True, True, True)
            with eng.Fori(1, TILES // 2 - 1) as j:
                step(j * 2, j, 0, True, True, True)
                step(j * 2 + 1, j, 1, True, True, True)
            for t in range(TILES - 2, TILES):
                step(t, t // 2, t % 2, True, t + 1 < TILES, t + 2 < TILES)

        def reused(eng, semaphore, t, per_tile=1):
            if not (isinstance(t, int) and t < 2):
                eng.wait_ge(semaphore, (t - 1) * per_tile)

        def emptied(eng, semaphore, t, per_tile=1):
            if not (isinstance(t, int) and t < 1):
                eng.wait_ge(semaphore, t * per_tile)

        def ffn_sweep(eng, step):
            for t in range(2):
                step(t, 0, t, t > 0, True, True)
            with eng.Fori(1, TILES // 2 - 1) as j:
                for b in range(2):
                    step(j * 2 + b, j, b, True, True, True)
            for t in range(TILES - 2, TILES):
                step(t, t // 2, t % 2, True, t + 1 < TILES, t + 2 < TILES)

        def at(buf, t):
            if isinstance(t, int):
                return buf[:, t, :]
            return buf[:, bass.ds(t, 1), :].rearrange("p a d -> p (a d)")

        block = stack.enter_context(nc.Block())

        @block.sync
        def _(sp):
            for n, w in enumerate((wq, wk, wv, wo)):
                sp.dma_start(weights[:, n, :], w).then_inc(w_loaded, 16)
            sp.dma_start(ident[:, :], ident_in).then_inc(w_loaded, 16)
            for n, v in enumerate((bq, bk, bv)):
                sp.dma_start(bias_cols[:, n:n + 1], v.rearrange("(d a) -> d a", a=1)).then_inc(w_loaded, 16)
            sp.dma_start(head_mask[:, :], head_mask_in).then_inc(w_loaded, 16)
            sp.dma_start(value_mask[:, :], value_mask_in).then_inc(w_loaded, 16)
            sp.dma_start(bo_rows[:, :], bo.rearrange("(a d) -> a d", a=1).broadcast_to([P, D])).then_inc(w_loaded, 16)

            def load_ctx(t, b):
                reused(sp, xc_transposed, t)
                sp.dma_start(ctx_sb[b][:, :], ctx_view[t]).then_inc(ctx_loaded[b], 16)

            load_ctx(0, 0)
            load_ctx(1, 1)
            with sp.Fori(1, TILES // 2) as j:
                for b in range(2):
                    sp.wait_ge(xc_transposed, j * 2 + b - 1)
                    sp.dma_start(ctx_sb[b][:, :], ctx_view[bass.ds(j * 2 + b, 1)].rearrange("a p d -> (a p) d")
                                 ).then_inc(ctx_loaded[b], 16)
            def store(t, b):
                sp.wait_ge(added, t + 1)
                rows = out_view[:, t, :] if isinstance(t, int) else out_view[:, bass.ds(t, 1), :].rearrange("p a d -> p (a d)")
                sp.dma_start(rows, result[b][:, :]).then_inc(stored[b], 16)

            with sp.Fori(0, TILES // 2) as j:
                store(j * 2, 0)
                store(j * 2 + 1, 1)
            for b in range(2):
                sp.wait_ge(stored[b], 16 * TILES // 2)

        @block.gpsimd
        def _(pool):
            pool.memset(minus_half[:, :], -0.5).then_inc(pool_step, 1)
            pool.wait_ge(w_loaded, 16 * N_W)
            for b in range(2):
                for s in range(PAIR):
                    pool.tensor_copy(v_blocks[b][:, s, :, HD], value_mask[:, :]).then_inc(ones_ready, 1)
            pool.wait_ge(stats_step, 2 * TILES)
            pool.tensor_scalar(rstd[:, :], mean_var[:, :, 1], EPS, None, ALU.add).then_inc(pool_step, 1)
            pool.wait_ge(pool_step, 2)
            pool.tensor_tensor(rstd[:, :], rstd[:, :], minus_half[:, :], ALU.pow).then_inc(rstd_ready, 1)
            pool.wait_ge(gate_ready, 1)
            pool.tensor_tensor(bo_rows[:, :], bo_rows[:, :], gate[:, 0:1].broadcast_to([P, D]), ALU.mult
                               ).then_inc(pool_step, 1)

            def mask_keys(t, b):
                pool.wait_ge(qk_ready, (t + 1) * 2)
                reused(pool, scored, t)
                pool.tensor_tensor(
                    k_masked[b][:, :, :, :],
                    k_t[b][:, :].rearrange("p (s a k) -> p s a k", s=PAIR, a=1).broadcast_to([P, PAIR, HG, S]),
                    head_mask[:, :].rearrange("p (a h c) -> p a h c", a=1, c=1).broadcast_to([P, PAIR, HG, S]),
                    ALU.mult).then_inc(k_masked_ready, 1)

            mask_keys(0, 0)
            pool.wait_ge(pool_step, 3)
            pool.tensor_tensor(x_biased[:, :, :], x_all[:, :, :],
                               bo_rows[:, :].rearrange("p (a d) -> p a d", a=1).broadcast_to([P, TILES, D]),
                               ALU.add).then_inc(xb_ready, 1)
            mask_keys(1, 1)

            def step(t, half, b, prev, next1, next2):
                if next2:
                    mask_keys(t + 2, b)

            attention_sweep(pool, step)

            pool.wait_ge(ffn_stats, 2 * TILES)
            pool.tensor_scalar(rstd[:, :], mean_var[:, :, 1], 1.0 + EPS, EPS * EPS, ALU.mult, ALU.add
                               ).then_inc(pool_step, 1)
            pool.wait_ge(pool_step, 4)
            pool.tensor_tensor(rstd[:, :], rstd[:, :], minus_half[:, :], ALU.pow).then_inc(ffn_rstd, 1)

            def split(t, b):
                pool.wait_ge(copied, sims_job(t) + 1)
                if not (isinstance(t, int) and t < 2):
                    pool.wait_ge(copied, parts_job(t - 2) + 1)
                flat = sims[b][:, :, :]
                hi = parts[b][:, :, :, 0, :].rearrange("p h s k -> p (h s) k")
                lo = parts[b][:, :, :, 1, :].rearrange("p h s k -> p (h s) k")
                pool.tensor_tensor(lo, flat, hi, ALU.subtract).then_inc(parts_ready, 1)

            def add_input(t, half, b):
                pool.wait_ge(copied, (LAST_JOB if isinstance(t, int) and t == TILES - 1 else job(t + 1, "x")) + 1)
                if not (isinstance(t, int) and t < 2):
                    pool.wait_ge(stored[b], half * 16)
                pool.tensor_tensor(result[b][:, :], ffn_y[b][:, :], at(x2_all, t), ALU.add).then_inc(added, 1)

            split(0, 0)

            def ffn_step(t, half, b, prev, next1, next2):
                if next1:
                    split(t + 1, 1 - b)
                if prev:
                    add_input(t - 1, half - (1 - b), 1 - b)

            ffn_sweep(pool, ffn_step)
            add_input(TILES - 1, (TILES - 1) // 2, (TILES - 1) % 2)

        @block.scalar
        def _(act):
            act.dma_start(x_all[:, :, :], x_view).then_inc(x_loaded, 16)
            act.dma_start(stage[:, :, :], wq_ffn.rearrange("d (n c) -> d n c", c=P)).then_inc(ffn_loaded, 16)
            act.dma_start(keys_sb[:, :, :, :], keys.rearrange("(g h) k s c -> (h k) g s c", g=FH * NK // P)).then_inc(ffn_loaded, 16)
            act.dma_start(down_sb[:, :, :], down.rearrange("(c p) d -> p c d", p=P)).then_inc(ffn_loaded, 16)
            act.dma_start(up_sb[:, :, :], up.rearrange("(c p) d -> p c d", p=P)).then_inc(ffn_loaded, 16)
            act.dma_start(norm_col[:, :], norm_w.rearrange("(d a) -> d a", a=1)).then_inc(ffn_loaded, 16)
            for n, g in enumerate((g_attn, g_ffn)):
                act.dma_start(gate_in[:, n:n + 1], g.rearrange("(a d) -> a d", a=1).broadcast_to([P, 1])
                              ).then_inc(x_loaded, 16)
            act.wait_ge(x_loaded, 48)
            act.activation(gate[:, :], gate_in[:, :], ACT.Tanh).then_inc(gate_ready, 1)
            act.wait_ge(w_transposed, 1)
            act.copy(weights_t[:, 0:3, :], ps_qk[:, 0:3, :]).then_inc(w_ready, 1)
            act.wait_ge(gate_ready, 1)
            act.activation(weights_t[:, 3, :], ps_qk[:, 3, :], ACT.Copy, scale=gate[:, 0:1]).then_inc(w_ready, 1)

            def copy_xc(t, b):
                act.wait_ge(xc_transposed, t + 1)
                reused(act, projected, t)
                act.copy(x_t[b][:, :], x_t_ps).then_inc(xc_ready, 1)
                act.copy(ctx_t[b][:, :, :, :],
                         ctx_t_ps.rearrange("p (s a k) -> p s a k", s=PAIR, a=1)
                         .broadcast_to([P, PAIR, 2, S])).then_inc(xc_ready, 1)

            def copy_qk(t, b):
                act.wait_ge(projected, t + 1)
                reused(act, scored, t)
                reused(act, k_masked_ready, t)
                act.activation(q_t[b][:, :], ps_qk[:, 0, :], ACT.Identity, bias=bias_cols[:, 0:1]).then_inc(qk_ready, 1)
                act.activation(k_t[b][:, :], ps_qk[:, 1, :], ACT.Identity, bias=bias_cols[:, 1:2]).then_inc(qk_ready, 1)

            def exponents(t, b):
                act.wait_ge(shift_done, t + 1)
                reused(act, probs_transposed, t)
                act.activation(probs[b][:, :], shifted[b][:, :], ACT.Exp, scale=SCALE).then_inc(exp_done, 1)

            copy_xc(0, 0)
            copy_qk(0, 0)
            copy_xc(1, 1)
            copy_qk(1, 1)
            exponents(0, 0)

            def step(t, half, b, prev, next1, next2):
                act.wait_ge(probs_transposed, t + 1)
                reused(act, mixed, t)
                act.copy(probs_t[b][:, :, :], probs_t_ps[:, :, :]).then_inc(probs_t_ready, 1)
                if prev:
                    copy_mixed(t - 1, 1 - b, t + 2 if next2 else None)
                if next2:
                    copy_xc(t + 2, b)
                    copy_qk(t + 2, b)
                if next1:
                    exponents(t + 1, 1 - b)

            def copy_mixed(t, b, joined=None):
                act.wait_ge(mixed_transposed, t + 1)
                if joined is not None:
                    act.wait_ge(xc_transposed, joined + 1)
                reused(act, attn_out, t)
                act.activation(mixed_t[b][:, :], mix_t_ps, ACT.Identity, bias=bias_cols[:, 2:3]
                               ).then_inc(mixed_t_ready, 1)

            attention_sweep(act, step)
            copy_mixed(TILES - 1, (TILES - 1) % 2)

            act.wait_ge(filled, KEYS_JOB + 1)
            act.copy(keys_t[:, :, :].rearrange("p n c -> p (n c)"), ring[0][:, 0:4 * P]).then_inc(copied, 1)
            for half in range(2):
                act.wait_ge(filled, WQ_JOB + half + 1)
                act.copy(wq_t[:, half * 8:half * 8 + 8, :].rearrange("p n c -> p (n c)"), ring[WQ_JOB + half]
                         ).then_inc(copied, 1)
            act.dma_start(stage[:, 0:E // P, :].rearrange("p n c -> p (n c)"), select_in).then_inc(sel_loaded, 16)
            act.wait_ge(ffn_loaded, 16 * 5)
            act.wait_ge(filled, DOWN_JOB + 1)
            act.activation(down_t[:, :, :].rearrange("p n c -> p (n c)"), ring[0], ACT.Copy, scale=norm_col[:, 0:1]
                           ).then_inc(copied, 1)
            act.wait_ge(filled, KEY_W_JOB + 1)
            act.activation(key_w[:, :], ring[1][:, 0:LISTS * NK], ACT.Copy, scale=norm_col[:, 0:1]).then_inc(copied, 1)
            act.wait_ge(sel_loaded, 16)
            act.copy(select[:, :], stage[:, 0:E // P, :].rearrange("p n c -> p (n c)")).then_inc(setup_ready, 1)

            def copy_turned(t, b, n):
                if not (isinstance(t, int) and t < 2):
                    act.wait_ge(filled, hidden_job(t - 2) + 1)
                act.copy(fn_t[b][:, :], ring[n][:, 0:P]).then_inc(copied, 1)

            def copy_sims(t, b, n):
                act.wait_ge(filled, sims_job(t) + 1)
                if not (isinstance(t, int) and t < 2):
                    act.wait_ge(least_ready, t - 1)
                    act.wait_ge(parts_ready, t - 1)
                    act.wait_ge(filled, parts_job(t - 2) + 1)
                act.copy(parts[b][:, :, :, 0, :].rearrange("p h s k -> p (h s) k").bitcast(F32R),
                         ring[n][:, 0:LISTS * NK].rearrange("p (n k) -> p n k", k=NK))
                act.copy(sims[b][:, :, :].rearrange("p n k -> p (n k)"), ring[n][:, 0:LISTS * NK]).then_inc(copied, 1)

            def gelu(t, b, n):
                act.wait_ge(filled, hidden_job(t) + 1)
                if not (isinstance(t, int) and t < 2):
                    act.wait_ge(y_ready, t - 1)
                act.activation(hidden[b][:, :], ring[n], ACT.Gelu).then_inc(copied, 1)

            def copy_parts(t, b, n):
                act.wait_ge(filled, parts_job(t) + 1)
                if not (isinstance(t, int) and t < 2):
                    act.wait_ge(filled, job(t - 2, "S7") + 1)
                act.copy(parts_t[b][:, :, :].rearrange("p n t -> p (n t)"), ring[n]).then_inc(copied, 1)

            def copy_excess(t, h, b):
                act.wait_ge(filled, job(t, f"S{h}") + 1)
                if h == 0:
                    act.wait_ge(least_ready, t + 1)
                if not (isinstance(t, int) and t < 1 and h < DEEP):
                    act.wait_ge(head_summed, t * FH + (h - DEEP + 1))
                act.activation(excess[h % DEEP][:, :], ring[slot(t, f"S{h}")], ACT.Relu, bias=least_neg[b][:, h:h + 1]
                               ).then_inc(copied, 1)

            for t in range(2):
                act.wait_ge(filled, turn_job(t) + 1)
                copy_turned(t, t, turn_job(t) % 3)
                copy_sims(t, t, sims_job(t) % 3)
            gelu(0, 0, hidden_job(0) % 3)
            copy_parts(0, 0, parts_job(0) % 3)

            def ffn_step(t, half, b, prev, next1, next2):
                copy_excess(t, 0, b)
                copy_excess(t, 1, b)
                copy_excess(t, 2, b)
                if next1:
                    gelu(t + 1, 1 - b, slot(t, "hid"))
                act.wait_ge(filled, job(t, "x") + 1)
                if prev:
                    if not (isinstance(t, int) and t < 3):
                        act.wait_ge(added, t - 2)
                    y = act.copy(ffn_y[1 - b][:, :], ring[slot(t, "x")][:, 512:512 + D])
                    if not next2:
                        y.then_inc(copied, 1)
                if next2:
                    copy_turned(t + 2, b, slot(t, "x"))
                copy_excess(t, 3, b)
                if next2:
                    copy_sims(t + 2, b, slot(t, "sim"))
                copy_excess(t, 4, b)
                copy_excess(t, 5, b)
                if next1:
                    copy_parts(t + 1, 1 - b, slot(t, "split"))
                copy_excess(t, 6, b)
                copy_excess(t, 7, b)

            ffn_sweep(act, ffn_step)
            act.wait_ge(filled, LAST_JOB + 1)
            act.wait_ge(added, TILES - 2)
            act.copy(ffn_y[(TILES - 1) % 2][:, :], ring[(LAST_JOB) % 3][:, 512:512 + D]).then_inc(copied, 1)

        @block.vector
        def _(dve):
            for b in range(2):
                dve.memset(v_blocks[b][:, :, :, 0:HD], 0.0).then_inc(ones_ready, 1)
            dve.wait_ge(x_loaded, 48)
            for t in range(TILES):
                dve.bn_stats(stats[:, t, :], x_all[:, t, :]).then_inc(stats_step, 1)
            dve.wait_ge(stats_step, TILES)
            for t in range(TILES):
                dve.bn_aggr(mean_var[:, t, :], stats[:, t, :]).then_inc(stats_step, 1)
            dve.wait_ge(stats_step, 2 * TILES)
            dve.wait_ge(rstd_ready, 1)

            def normalise(t, b):
                reused(dve, xc_transposed, t)
                mean = at(mean_var, t)[:, 0:1]
                scale = rstd[:, t:t + 1] if isinstance(t, int) else rstd[:, bass.ds(t, 1)]
                dve.tensor_scalar(xn[b][:, :], at(x_all, t), mean, scale, ALU.subtract, ALU.mult
                                  ).then_inc(xn_ready, 1)

            def block_values(t, b):
                dve.wait_ge(projected, t + 1)
                reused(dve, mixed, t)
                dve.tensor_tensor(
                    v_blocks[b][:, :, :, 0:HD],
                    ps_v[:, 0:PAIR, :].rearrange("p s (h e) -> p s h e", h=H),
                    value_mask[:, :].rearrange("p (a h c) -> p a h c", a=1, c=1).broadcast_to([P, PAIR, H, HD]),
                    ALU.mult).then_inc(v_ready, 1)

            def shift(t, b):
                dve.wait_ge(scored, t + 1)
                dve.tensor_reduce(row_max[:, :], scores_ps[:, :, :].rearrange("p g (h k) -> p g h k", h=HG), AX.X, ALU.max
                                  ).then_inc(max_ready, 1)
                dve.wait_ge(max_ready, t + 1)
                reused(dve, exp_done, t)
                dve.tensor_tensor(
                    shifted[b][:, :].rearrange("p (g h k) -> p g h k", g=G, h=HG),
                    scores_ps[:, :, :].rearrange("p g (h k) -> p g h k", h=HG),
                    row_max[:, :].rearrange("p (g h a) -> p g h a", g=G, a=1).broadcast_to([P, G, HG, S]),
                    ALU.subtract).then_inc(shift_done, 1)

            def divide(t, b):
                dve.wait_ge(mixed, t + 1)
                mix = mix_ps.rearrange("p (h e) -> p h e", h=H)
                dve.reciprocal(row_rec[:, :], mix[:, :, HD]).then_inc(rec_ready, 1)
                dve.wait_ge(rec_ready, t + 1)
                reused(dve, mixed_transposed, t)
                dve.tensor_tensor(mixed_sb[b][:, :].rearrange("p (h e) -> p h e", h=H), mix[:, :, 0:HD],
                                  row_rec[:, :].rearrange("p (h a) -> p h a", a=1).broadcast_to([P, H, HD]),
                                  ALU.mult).then_inc(mixed_ready, 1)

            def residual(t):
                dve.wait_ge(attn_out, t + 1)
                dve.tensor_tensor(at(x2_all, t), y_ps, at(x_biased, t), ALU.add).then_inc(x2_ready, 1)

            normalise(0, 0)
            normalise(1, 1)
            dve.wait_ge(ones_ready, 2 + 2 * PAIR)
            block_values(0, 0)
            block_values(1, 1)
            shift(0, 0)
            dve.wait_ge(xb_ready, 1)

            def step(t, half, b, prev, next1, next2):
                if next2:
                    normalise(t + 2, b)
                if prev:
                    divide(t - 1, 1 - b)
                if next1:
                    shift(t + 1, 1 - b)
                if prev:
                    residual(t - 1)
                if next2:
                    block_values(t + 2, b)

            attention_sweep(dve, step)
            divide(TILES - 1, (TILES - 1) % 2)
            residual(TILES - 1)

            dve.wait_ge(ffn_loaded, 16 * 5)
            dve.tensor_scalar(up_sb[:, :, :], up_sb[:, :, :], gate[:, 1:2], None, ALU.mult).then_inc(setup_ready, 1)
            dve.wait_ge(x2_ready, TILES)
            for t in range(TILES):
                dve.bn_stats(stats[:, t, :], x2_all[:, t, :]).then_inc(ffn_stats, 1)
            dve.wait_ge(ffn_stats, TILES)
            for t in range(TILES):
                dve.bn_aggr(mean_var[:, t, :], stats[:, t, :]).then_inc(ffn_stats, 1)
            dve.wait_ge(ffn_stats, 2 * TILES)
            dve.wait_ge(ffn_rstd, 1)

            def normalise_ffn(t, b):
                if not (isinstance(t, int) and t < 2):
                    dve.wait_ge(copied, turn_job(t - 2) + 1)
                mean = at(mean_var, t)[:, 0:1]
                scale = rstd[:, t:t + 1] if isinstance(t, int) else rstd[:, bass.ds(t, 1)]
                dve.tensor_scalar(fn[b][:, :], at(x2_all, t), mean, scale, ALU.subtract, ALU.mult
                                  ).then_inc(fn_ready, 1)

            GROUPS = 10

            def group_done(t, n):
                dve.wait_ge(ranked, t * GROUPS + n)

            halves = (range(0, LISTS // 2), range(LISTS // 2, LISTS))

            def rank_first(t, b, half):
                for n in halves[half]:
                    last = dve.max(top[:, n, 0:8], sims[b][:, n, :])
                last.then_inc(ranked, 1)

            def rank_strike(t, b, half):
                for n in halves[half]:
                    last = dve.match_replace(struck[:, n, :], top[:, n, 0:8], sims[b][:, n, :], LOWEST)
                last.then_inc(ranked, 1)

            def rank_second(t, half):
                for n in halves[half]:
                    last = dve.max(top[:, n, 8:16], struck[:, n, :])
                last.then_inc(ranked, 1)

            def candidates(t):
                sides = top[:, :, :].rearrange("p (h s) k -> p h s k", s=SIDES)
                start, a = 0, 0
                while a < K:
                    width = REACH[a]
                    rows = REACH.count(width)
                    last = dve.tensor_tensor(
                        cand[:, :, start:start + rows * width].rearrange("p h (a b) -> p h a b", b=width),
                        sides[:, :, 0, a:a + rows].rearrange("p h (a b) -> p h a b", b=1).broadcast_to([P, FH, rows, width]),
                        sides[:, :, 1, 0:width].rearrange("p h (a b) -> p h a b", a=1).broadcast_to([P, FH, rows, width]),
                        ALU.add)
                    start += rows * width
                    a += rows
                last.then_inc(ranked, 1)

            def best_first():
                for h in range(FH):
                    last = dve.max(best[:, h, 0:8], cand[:, h, :])
                last.then_inc(ranked, 1)

            def best_strike():
                for h in range(FH):
                    last = dve.match_replace(cand_struck[:, h, :], best[:, h, 0:8], cand[:, h, :], LOWEST)
                last.then_inc(ranked, 1)

            def best_second():
                for h in range(FH):
                    last = dve.max(best[:, h, 8:16], cand_struck[:, h, :])
                last.then_inc(ranked, 1)

            def least_score(t, b):
                if not (isinstance(t, int) and t < 2):
                    dve.wait_ge(copied, job(t - 2, "S7") + 1)
                dve.tensor_scalar(least[b][:, :], best[:, :, K - 1], BELOW, 0.0, ALU.mult, ALU.max).then_inc(least_step, 1)
                dve.wait_ge(least_step, t + 1)
                dve.tensor_scalar(least_neg[b][:, :], least[b][:, :], -1.0, None, ALU.mult).then_inc(least_ready, 1)

            def head_base(t, h, b):
                dve.wait_ge(copied, job(t, f"S{h}") + 1)
                if not (isinstance(t, int) and t < 1 and h < DEEP):
                    dve.wait_ge(head_summed, t * FH + (h - DEEP + 1))
                dve.tensor_scalar(base[h % DEEP][:, :], excess[h % DEEP][:, :], 0.0, least[b][:, h:h + 1], ALU.is_gt, ALU.mult
                                  ).then_inc(base_ready, 1)

            def weigh(t, b):
                dve.wait_ge(head_summed, (t + 1) * FH)
                dve.wait_ge(copied, hidden_job(t) + 1)
                if not (isinstance(t, int) and t < 1):
                    dve.wait_ge(filled, job(t, "x") + 1)
                dve.tensor_tensor(mix_y[:, :, :].rearrange("p n t -> p (n t)"), mix_w_ps, hidden[b][:, :], ALU.mult
                                  ).then_inc(y_ready, 1)

            def rank_wait(t, n):
                if n == 0:
                    dve.wait_ge(copied, sims_job(t) + 1)
                if n >= 2:
                    group_done(t, (1, 3, 4, 7, 8, 9)[n - 2])

            def rank(t, b, n):
                if n == 0:
                    rank_first(t, b, 0)
                if n == 1:
                    rank_first(t, b, 1)
                if n == 2:
                    rank_strike(t, b, 0)
                if n == 3:
                    rank_strike(t, b, 1)
                    rank_second(t, 0)
                if n == 4:
                    rank_second(t, 1)
                    group_done(t, 6)
                    candidates(t)
                if n == 5:
                    best_first()
                if n == 6:
                    best_strike()
                if n == 7:
                    best_second()
                    group_done(t, 10)
                    least_score(t, b)

            normalise_ffn(0, 0)
            normalise_ffn(1, 1)
            for n in range(8):
                rank_wait(0, n)
                rank(0, 0, n)

            def ffn_step(t, half, b, prev, next1, next2):
                if next2:
                    normalise_ffn(t + 2, b)
                if prev:
                    weigh(t - 1, 1 - b)
                for h in range(FH):
                    if next1:
                        rank_wait(t + 1, h)
                    head_base(t, h, b)
                    if next1:
                        rank(t + 1, 1 - b, h)

            ffn_sweep(dve, ffn_step)
            weigh(TILES - 1, (TILES - 1) % 2)

        @block.tensor
        def _(pe):
            pe.wait_ge(w_loaded, 16 * N_W)
            for n in range(4):
                mm = pe.transpose(ps_qk[:, n, :], weights[:, n, :], ident[:, :])
            mm.then_inc(w_transposed, 1)

            def transpose_xc(t, half, b):
                pe.wait_ge(xn_ready, t + 1)
                pe.wait_ge(ctx_loaded[b], (half + 1) * 16)
                emptied(pe, xc_ready, t, 2)
                pe.transpose(x_t_ps, xn[b][:, :], ident[:, :])
                pe.transpose(ctx_t_ps, ctx_sb[b][:, :], ident[:, :]).then_inc(xc_transposed, 1)

            def project(t, b):
                pe.wait_ge(xc_ready, (t + 1) * 2)
                emptied(pe, qk_ready, t, 2)
                emptied(pe, v_ready, t)
                pe.matmul(ps_qk[:, 0, :], weights_t[:, 0, :], x_t[b][:, :], start=True, stop=True)
                pe.matmul(ps_qk[:, 1, :], weights_t[:, 1, :], ctx_t[b][:, :, 0, :], start=True, stop=True)
                for s in range(PAIR):
                    twice = ctx_t[b][:, s, :, :].rearrange("p a k -> p (a k)")
                    mm = pe.matmul(ps_v[:, s, :], twice, weights_t[:, 2, :], start=True, stop=True)
                mm.then_inc(projected, 1)

            def score(t, b):
                for g in range(G):
                    rows = slice(g * P // G, (g + 1) * P // G)
                    for s in range(PAIR):
                        mm = pe.matmul(scores_ps[s * S:(s + 1) * S, g, :], q_t[b][rows, s * S:(s + 1) * S],
                                       k_masked[b][rows, s, :, :], start=True, stop=True)
                mm.then_inc(scored, 1)

            def transpose_mixed(t, b, joined=None):
                pe.wait_ge(mixed_ready, t + 1)
                pe.wait_ge(xc_ready, t * 2 + 6 if joined is not None else TILES * 2)
                emptied(pe, mixed_t_ready, t)
                pe.transpose(mix_t_ps, mixed_sb[b][:, :], ident[:, :]).then_inc(mixed_transposed, 1)

            def output(t, b):
                pe.wait_ge(mixed_t_ready, t + 1)
                emptied(pe, x2_ready, t)
                pe.matmul(y_ps, mixed_t[b][:, :], weights_t[:, 3, :], start=True, stop=True).then_inc(attn_out, 1)

            pe.wait_ge(w_ready, 2)
            transpose_xc(0, 0, 0)
            transpose_xc(1, 0, 1)
            project(0, 0)
            project(1, 1)
            pe.wait_ge(k_masked_ready, 1)
            score(0, 0)

            def step(t, half, b, prev, next1, next2):
                if next1:
                    pe.wait_ge(k_masked_ready, t + 2)
                pe.wait_ge(exp_done, t + 1)
                emptied(pe, probs_t_ready, t)
                for p in range(HP):
                    mm = pe.transpose(probs_t_ps[:, p, :],
                                      probs[b][:, p * P:(p + 1) * P], ident[:, :])
                mm.then_inc(probs_transposed, 1)
                if prev:
                    transpose_mixed(t - 1, 1 - b, t + 2 if next2 else None)
                if next2:
                    transpose_xc(t + 2, half + 1, b)
                if next1:
                    score(t + 1, 1 - b)
                if prev:
                    output(t - 1, 1 - b)
                if next2:
                    project(t + 2, b)
                pe.wait_ge(probs_t_ready, t + 1)
                pe.wait_ge(v_ready, t + 1)
                if prev:
                    pe.wait_ge(x2_ready, t)
                for p in range(HP):
                    for s in range(PAIR):
                        mm = pe.matmul(mix_ps[s * S:(s + 1) * S, 2 * VW * p:2 * VW * (p + 1)],
                                       probs_t[b][:, p, s * S:(s + 1) * S],
                                       v_blocks[b][:, s, 2 * p:2 * p + 2, :], start=True, stop=True)
                mm.then_inc(mixed, 1)

            attention_sweep(pe, step)
            transpose_mixed(TILES - 1, (TILES - 1) % 2)
            output(TILES - 1, (TILES - 1) % 2)

            pe.wait_ge(x2_ready, TILES)
            pe.wait_ge(ffn_loaded, 16 * 5)
            for g in range(2):
                for side in range(SIDES):
                    mm = pe.transpose(ring[0][:, (g * SIDES + side) * P:(g * SIDES + side + 1) * P], keys_sb[:, g, side, :],
                                      ident[:, :])
            mm.then_inc(filled, 1)
            for n in range(LISTS):
                mm = pe.transpose(ring[WQ_JOB + n // 8][:, n % 8 * P:(n % 8 + 1) * P], stage[:, n, :], ident[:, :])
                if n % 8 == 7:
                    mm.then_inc(filled, 1)
            pe.wait_ge(copied, KEYS_JOB + 1)
            for c in range(EC):
                mm = pe.transpose(ring[0][:, c * P:(c + 1) * P], down_sb[:, c, :], ident[:, :])
            mm.then_inc(filled, 1)
            pe.wait_ge(copied, WQ_JOB + 2)
            for h in range(FH):
                for side in range(SIDES):
                    n = h * SIDES + side
                    per = P // NK
                    mm = pe.matmul(ring[1][:, n * NK:(n + 1) * NK], wq_t[:, n, :],
                                   keys_t[:, h // per * SIDES + side, h % per * NK:(h % per + 1) * NK],
                                   start=True, stop=True)
            mm.then_inc(filled, 1)
            pe.wait_ge(setup_ready, 2)

            def ring_free(n):
                pe.wait_ge(copied, n - 2)

            def turn_input(t, b, n, last=True):
                pe.wait_ge(fn_ready, t + 1)
                pe.transpose(ring[n][:, 0:P], fn[b][:, :], ident[:, :]).then_inc(filled, 1)

            def similarities(t, b, n):
                pe.wait_ge(copied, turn_job(t) + 1)
                pe.matmul(ring[n][:, 0:LISTS * NK], fn_t[b][:, :], key_w[:, :], start=True, stop=True).then_inc(filled, 1)

            def experts(t, b, n):
                pe.wait_ge(copied, turn_job(t) + 1)
                for c in range(EC):
                    mm = pe.matmul(ring[n][:, c * P:(c + 1) * P], down_t[:, c, :], fn_t[b][:, :], start=True, stop=True)
                mm.then_inc(filled, 1)

            def turn_parts(t, b, n):
                pe.wait_ge(parts_ready, t + 1)
                for h in range(FH):
                    mm = pe.transpose(ring[n][:, h * P:(h + 1) * P], parts[b][:, h, :, :, :].rearrange("p s a k -> p (s a k)"),
                                      ident[:, :])
                mm.then_inc(filled, 1)

            def pair_scores(t, h, b):
                ring_free(job(t, f"S{h}"))
                if h == 0:
                    pe.wait_ge(copied, parts_job(t) + 1)
                for half in range(2):
                    cols = slice(half * 512, half * 512 + 512)
                    mm = pe.matmul(ring[slot(t, f"S{h}")][:, cols], parts_t[b][:, h, :], select[:, cols], start=True, stop=True)
                mm.then_inc(filled, 1)

            def sum_head(t, h):
                pe.wait_ge(base_ready, t * FH + h + 1)
                if h == 0 and not (isinstance(t, int) and t < 1):
                    pe.wait_ge(y_ready, t)
                for part, score in enumerate((excess[h % DEEP], base[h % DEEP])):
                    for c in range(EC):
                        first = h == 0 and part == 0 and c % 4 == 0
                        mm = pe.matmul(mix_w_ps[:, c * P:(c + 1) * P], score[:, c * P:(c + 1) * P], ident[:, :],
                                       is_transpose=True, start=first, stop=(h == FH - 1 and part == 1 and c % 4 == 3),
                                       skip_group_check=True)
                mm.then_inc(head_summed, 1)

            def ffn_out(t, n):
                pe.wait_ge(y_ready, t + 1)
                for c in range(EC):
                    mm = pe.matmul(ring[n][:, 512:512 + D], mix_y[:, c, :], up_sb[:, c, :], start=(c == 0), stop=(c == EC - 1))
                return mm

            for t in range(2):
                ring_free(turn_job(t))
                turn_input(t, t, turn_job(t) % 3)
                ring_free(sims_job(t))
                similarities(t, t, sims_job(t) % 3)
            ring_free(hidden_job(0))
            experts(0, 0, hidden_job(0) % 3)
            ring_free(parts_job(0))
            turn_parts(0, 0, parts_job(0) % 3)

            def ffn_step(t, half, b, prev, next1, next2):
                pair_scores(t, 0, b)
                pair_scores(t, 1, b)
                if prev:
                    sum_head(t - 1, 7)
                pair_scores(t, 2, b)
                if next1:
                    ring_free(job(t, "hid"))
                    experts(t + 1, 1 - b, slot(t, "hid"))
                ring_free(job(t, "x"))
                if prev:
                    mm = ffn_out(t - 1, slot(t, "x"))
                    if not next2:
                        mm.then_inc(filled, 1)
                if next2:
                    turn_input(t + 2, b, slot(t, "x"))
                sum_head(t, 0)
                pair_scores(t, 3, b)
                sum_head(t, 1)
                if next2:
                    ring_free(job(t, "sim"))
                    similarities(t + 2, b, slot(t, "sim"))
                pair_scores(t, 4, b)
                sum_head(t, 2)
                pair_scores(t, 5, b)
                sum_head(t, 3)
                if next1:
                    ring_free(job(t, "split"))
                    turn_parts(t + 1, 1 - b, slot(t, "split"))
                sum_head(t, 4)
                pair_scores(t, 6, b)
                sum_head(t, 5)
                pair_scores(t, 7, b)
                sum_head(t, 6)

            ffn_sweep(pe, ffn_step)
            sum_head(TILES - 1, 7)
            ring_free(LAST_JOB)
            ffn_out(TILES - 1, LAST_JOB % 3).then_inc(filled, 1)


def kernel(x, ctx_1024, g_xattn, g_ffn, L0_xattn_Wq, L0_xattn_bq, L0_xattn_Wk, L0_xattn_bk, L0_xattn_Wv,
           L0_xattn_bv, L0_xattn_Wo, L0_xattn_bo, L0_ffn_norm_w, L0_ffn_wq, L0_ffn_keys,
           L0_ffn_expert_down, L0_ffn_expert_up):
    import numpy as np
    import concourse.bacc as bacc
    from concourse.bass_utils import run_bass_kernel_spmd

    partition, expert = np.arange(P)[:, None], np.arange(E)
    side, key = partition // (2 * NK), partition % NK
    constants = {
        "ident": np.eye(P, dtype=np.float32),
        "head_mask": (partition % (P // G) // HD == np.arange(HG)).astype(np.float32),
        "value_mask": (partition // S == np.arange(H) % 2).astype(np.float32),
        "select": (np.where(side == 0, expert // NK, expert % NK) == key).astype(np.float32),
    }
    arrays = dict(x=x, ctx=ctx_1024, g_attn=g_xattn, g_ffn=g_ffn, wq=L0_xattn_Wq, bq=L0_xattn_bq, wk=L0_xattn_Wk,
                  bk=L0_xattn_bk, wv=L0_xattn_Wv, bv=L0_xattn_bv, wo=L0_xattn_Wo, bo=L0_xattn_bo, norm_w=L0_ffn_norm_w,
                  wq_ffn=L0_ffn_wq, keys=L0_ffn_keys, down=L0_ffn_expert_down, up=L0_ffn_expert_up, **constants)
    nc = bacc.Bacc("TRN2", target_bir_lowering=False, num_devices=1)
    feeds, args = {}, []
    for name, a in arrays.items():
        a = np.ascontiguousarray(a)
        feeds[f"in_{name}"] = a
        args.append(nc.dram_tensor(f"in_{name}", a.shape, mybir.dt.from_np(a.dtype), kind="ExternalInput").ap())
    args.append(nc.dram_tensor("out_x", x.shape, F32, kind="ExternalOutput").ap())
    flamingo_kernel(nc, *args)
    return run_bass_kernel_spmd(nc, [feeds], core_ids=[0]).results[0]["out_x"]
```

```python
from contextlib import ExitStack

import concourse.bass as bass
from concourse import mybir

ALU = mybir.AluOpType
ACT = mybir.ActivationFunctionType
AX = mybir.AxisListType
F32 = mybir.dt.float32
F32R = mybir.dt.float32r

P = 128
B, S = 32, 64
D = 128
T = B * S
TILES = T // P
PAIR = P // S
H = 16
HD = D // H
G = 2
HG = H // G
HP = H // 2
VW = HD + 1
FH = 8
K = 16
NK = 32
SIDES = 2
LISTS = FH * SIDES
E = NK * NK
EC = E // P
REACH = [K // (a + 1) for a in range(K)]
CAND = sum(REACH)
ADDED = (1, 2, 4, 5, 6)
LOWEST = -3.0e38
BELOW = 1.0 - 2.0 ** -21
EPS = 1e-5
SCALE = float(HD) ** -0.5


def flamingo_kernel(nc, x, ctx_in, g_attn, g_ffn, wq, bq, wk, bk, wv, bv, wo, bo,
                    norm_w, wq_ffn, keys, down, up, ident_in, head_mask_in, value_mask_in, select_in, out):
    x_view = x.rearrange("(t two) s d -> (two s) t d", two=PAIR)
    ctx_view = ctx_in.rearrange("(t two) s d -> t (two s) d", two=PAIR)
    out_view = out.rearrange("(t two) s d -> (two s) t d", two=PAIR)

    with ExitStack() as stack:
        def sb(name, shape, dt=F32):
            return stack.enter_context(nc.sbuf_tensor(name, shape, dt))

        def ps(name, shape, dt=F32):
            return stack.enter_context(nc.psum_tensor(name, shape, dt))

        def sem(name):
            return stack.enter_context(nc.semaphore(name))

        ident = sb("ident", [P, P])
        head_mask = sb("head_mask", [P, HG])
        value_mask = sb("value_mask", [P, H])
        weights = sb("weights", [P, 4, D])
        weights_t = sb("weights_t", [P, 4, D])
        bias_rows = sb("bias_rows", [4, D])
        bias_cols = sb("bias_cols", [P, 4])
        gate_in = sb("gate_in", [P, 2])
        gate = sb("gate", [P, 2])
        bo_rows = sb("bo_rows", [P, D])
        minus_half = sb("minus_half", [P, TILES])

        x_all = sb("x_all", [P, TILES, D])
        x_biased = sb("x_biased", [P, TILES, D])
        x2_all = sb("x2_all", [P, TILES, D])
        stats = sb("stats", [P, TILES, 6])
        mean_var = sb("mean_var", [P, TILES, 2])
        rstd = sb("rstd", [P, TILES])

        ctx_sb = [sb(f"ctx_sb{b}", [P, D]) for b in range(2)]
        xn = [sb(f"xn{b}", [P, D]) for b in range(2)]
        x_t = [sb(f"x_t{b}", [P, P]) for b in range(2)]
        ctx_t = [sb(f"ctx_t{b}", [P, PAIR, 2, S]) for b in range(2)]
        q_t = [sb(f"q_t{b}", [P, P]) for b in range(2)]
        k_t = [sb(f"k_t{b}", [P, P]) for b in range(2)]
        k_masked = [sb(f"k_masked{b}", [P, PAIR, HG, S]) for b in range(2)]
        v_blocks = [sb(f"v_blocks{b}", [P, PAIR, H, VW]) for b in range(2)]
        row_max = sb("row_max", [P, H])
        shifted = [sb(f"shifted{b}", [P, H * S]) for b in range(2)]
        probs = [sb(f"probs{b}", [P, H * S]) for b in range(2)]
        probs_t = [sb(f"probs_t{b}", [P, HP, P]) for b in range(2)]
        row_rec = sb("row_rec", [P, H])
        mixed_sb = [sb(f"mixed_sb{b}", [P, D]) for b in range(2)]
        mixed_t = [sb(f"mixed_t{b}", [P, P]) for b in range(2)]

        banks = ps("banks", [P, 8, 512])
        ps_turned, ps_qk, ps_v = (banks[:, n, :].rearrange("p (n c) -> p n c", n=4) for n in range(3))
        scores_ps = banks[:, 4:6, :]
        probs_t_ps = banks[:, 6:8, :].rearrange("p n (m c) -> p (n m) c", c=P)
        ring = [banks[:, 2 * n:2 * n + 2, :].rearrange("p n c -> p (n c)") for n in range(3)]
        mix_w_ps = banks[:, 6:8, :].rearrange("p n c -> p (n c)")
        x_t_ps, ctx_t_ps, mix_t_ps = (ps_turned[:, n, :] for n in range(3))
        mix_ps = banks[:, 3, 0:H * VW]
        y_ps = ps_v[:, PAIR, :]

        select = sb("select", [P, E], F32R)
        norm_col = sb("norm_col", [P, 1])
        stage = sb("stage", [P, LISTS, P])
        keys_sb = sb("keys_sb", [P, FH * NK // P, SIDES, P])
        down_sb = sb("down_sb", [P, EC, D])
        up_sb = sb("up_sb", [P, EC, D])
        keys_t = sb("keys_t", [P, 2 * SIDES, P])
        wq_t = sb("wq_t", [P, LISTS, P])
        key_w = sb("key_w", [P, LISTS * NK])
        down_t = sb("down_t", [P, EC, P])

        fn = [sb(f"fn{b}", [P, D]) for b in range(2)]
        fn_t = [sb(f"fn_t{b}", [P, P]) for b in range(2)]
        sims = [sb(f"sims{b}", [P, LISTS, NK]) for b in range(2)]
        parts = [sb(f"parts{b}", [P, FH, SIDES, 2, NK]) for b in range(2)]
        parts_t = [sb(f"parts_t{b}", [P, FH, P], F32R) for b in range(2)]
        struck = sb("struck", [P, LISTS, NK])
        top = sb("top", [P, LISTS, K])
        cand = sb("cand", [P, FH, CAND])
        cand_struck = sb("cand_struck", [P, FH, CAND])
        best = sb("best", [P, FH, K])
        least = [sb(f"least{b}", [P, FH]) for b in range(2)]
        least_neg = [sb(f"least_neg{b}", [P, FH]) for b in range(2)]
        excess = [probs_t[n][:, :, :].rearrange("p n t -> p (n t)") for n in range(2)]
        excess += [buf[n][:, :] for buf in (shifted, probs) for n in range(2)]
        excess += [sb(f"excess{n}", [P, E])[:, :] for n in range(6, FH)]
        base = [sb(f"base{n}", [P, E]) for n in range(len(ADDED))]
        hidden = [sb(f"hidden{b}", [P, EC * P]) for b in range(2)]
        mix_y = sb("mix_y", [P, EC, P])
        ffn_y = [sb(f"ffn_y{b}", [P, D]) for b in range(2)]
        result = [sb(f"result{b}", [P, D]) for b in range(2)]

        ffn_loaded = sem("ffn_loaded")
        sel_loaded = sem("sel_loaded")
        filled = sem("filled")
        copied = sem("copied")
        setup_ready = sem("setup_ready")
        ffn_stats = sem("ffn_stats")
        ffn_rstd = sem("ffn_rstd")
        fn_ready = sem("fn_ready")
        parts_ready = sem("parts_ready")
        ranked = sem("ranked")
        least_step = sem("least_step")
        least_ready = sem("least_ready")
        base_ready = sem("base_ready")
        put_together = sem("put_together")
        head_summed = sem("head_summed")
        y_ready = sem("y_ready")
        added = sem("added")

        KEYS_JOB, WQ_JOB, DOWN_JOB, KEY_W_JOB = 0, 1, 3, 4
        FIRST = 10
        BODY = ("S0", "S1", "S2", "hid", "S3", "split", "S4", "S5", "x", "S6", "sim", "S7")
        ABSENT = {TILES - 2: ("sim",), TILES - 1: ("sim", "split")}

        def job(t, kind):
            at = BODY.index(kind)
            if not isinstance(t, int):
                return t * len(BODY) + (FIRST + at)
            missing = sum(len(kinds) for body, kinds in ABSENT.items() if body < t)
            missing += sum(BODY.index(kind) < at for kind in ABSENT.get(t, ()))
            return FIRST + t * len(BODY) + at - missing

        def slot(t, kind):
            return (job(t, kind) if isinstance(t, int) else FIRST + BODY.index(kind)) % 3

        LAST_JOB = job(TILES, "S0")

        def turn_job(tile):
            return (5, 7)[tile] if isinstance(tile, int) and tile < 2 else job(tile - 2, "x")

        def sims_job(tile):
            return (6, 8)[tile] if isinstance(tile, int) and tile < 2 else job(tile - 2, "sim")

        def hidden_job(tile):
            return job(tile, "hid")

        def parts_job(tile):
            return 9 if isinstance(tile, int) and tile < 1 else job(tile - 1, "split")

        w_loaded = sem("w_loaded")
        x_loaded = sem("x_loaded")
        ctx_loaded = [sem(f"ctx_loaded{b}") for b in range(2)]
        w_transposed = sem("w_transposed")
        w_ready = sem("w_ready")
        gate_ready = sem("gate_ready")
        stats_step = sem("stats_step")
        rstd_ready = sem("rstd_ready")
        pool_step = sem("pool_step")
        xb_ready = sem("xb_ready")
        ones_ready = sem("ones_ready")
        xn_ready = sem("xn_ready")
        xc_transposed = sem("xc_transposed")
        xc_ready = sem("xc_ready")
        projected = sem("projected")
        values_projected = sem("values_projected")
        qk_ready = sem("qk_ready")
        k_masked_ready = sem("k_masked_ready")
        v_ready = sem("v_ready")
        scored = sem("scored")
        max_ready = sem("max_ready")
        shift_done = sem("shift_done")
        exp_done = sem("exp_done")
        probs_transposed = sem("probs_transposed")
        probs_t_ready = sem("probs_t_ready")
        mixed = sem("mixed")
        rec_ready = sem("rec_ready")
        mixed_ready = sem("mixed_ready")
        mixed_transposed = sem("mixed_transposed")
        mixed_t_ready = sem("mixed_t_ready")
        attn_out = sem("attn_out")
        x2_ready = sem("x2_ready")
        stored = [sem(f"stored{b}") for b in range(2)]

        N_W = 4 + 1 + 1 + 2 + 3

        def attention_sweep(eng, step):
            for t in range(4):
                step(t, t // 2, t % 2)
            with eng.Fori(2, TILES // 2 - 2) as j:
                for b in range(2):
                    step(j * 2 + b, j, b)
            for t in range(TILES - 4, TILES + 3):
                step(t, t // 2, t % 2)

        def has(t):
            return not isinstance(t, int) or 0 <= t < TILES

        def reused(eng, semaphore, t, per_tile=1):
            if not (isinstance(t, int) and t < 2):
                eng.wait_ge(semaphore, (t - 1) * per_tile)

        def emptied(eng, semaphore, t, per_tile=1):
            if not (isinstance(t, int) and t < 1):
                eng.wait_ge(semaphore, t * per_tile)

        def ffn_sweep(eng, step):
            for t in range(2):
                step(t, 0, t, t > 0, True, True)
            with eng.Fori(1, TILES // 2 - 1) as j:
                for b in range(2):
                    step(j * 2 + b, j, b, True, True, True)
            for t in range(TILES - 2, TILES):
                step(t, t // 2, t % 2, True, t + 1 < TILES, t + 2 < TILES)

        def at(buf, t):
            if isinstance(t, int):
                return buf[:, t, :]
            return buf[:, bass.ds(t, 1), :].rearrange("p a d -> p (a d)")

        block = stack.enter_context(nc.Block())

        @block.sync
        def _(sp):
            for n, w in enumerate((wq, wk, wv, wo)):
                sp.dma_start(weights[:, n, :], w).then_inc(w_loaded, 16)
            sp.dma_start(ident[:, :], ident_in).then_inc(w_loaded, 16)
            for n, v in enumerate((bq, bk, bv)):
                sp.dma_start(bias_cols[:, n:n + 1], v.rearrange("(d a) -> d a", a=1)).then_inc(w_loaded, 16)
            sp.dma_start(head_mask[:, :], head_mask_in).then_inc(w_loaded, 16)
            sp.dma_start(value_mask[:, :], value_mask_in).then_inc(w_loaded, 16)
            sp.dma_start(bo_rows[:, :], bo.rearrange("(a d) -> a d", a=1).broadcast_to([P, D])).then_inc(w_loaded, 16)

            def load_ctx(t, b):
                reused(sp, xc_transposed, t)
                sp.dma_start(ctx_sb[b][:, :], ctx_view[t]).then_inc(ctx_loaded[b], 16)

            load_ctx(0, 0)
            load_ctx(1, 1)
            with sp.Fori(1, TILES // 2) as j:
                for b in range(2):
                    sp.wait_ge(xc_transposed, j * 2 + b - 1)
                    sp.dma_start(ctx_sb[b][:, :], ctx_view[bass.ds(j * 2 + b, 1)].rearrange("a p d -> (a p) d")
                                 ).then_inc(ctx_loaded[b], 16)
            def store(t, b):
                sp.wait_ge(added, t + 1)
                rows = out_view[:, t, :] if isinstance(t, int) else out_view[:, bass.ds(t, 1), :].rearrange("p a d -> p (a d)")
                sp.dma_start(rows, result[b][:, :]).then_inc(stored[b], 16)

            with sp.Fori(0, TILES // 2) as j:
                store(j * 2, 0)
                store(j * 2 + 1, 1)
            for b in range(2):
                sp.wait_ge(stored[b], 16 * TILES // 2)

        @block.gpsimd
        def _(pool):
            pool.memset(minus_half[:, :], -0.5).then_inc(pool_step, 1)
            pool.wait_ge(w_loaded, 16 * N_W)
            for b in range(2):
                for s in range(PAIR):
                    pool.tensor_copy(v_blocks[b][:, s, :, HD], value_mask[:, :]).then_inc(ones_ready, 1)
            pool.wait_ge(stats_step, 2 * TILES)
            pool.tensor_scalar(rstd[:, :], mean_var[:, :, 1], EPS, None, ALU.add).then_inc(pool_step, 1)
            pool.wait_ge(pool_step, 2)
            pool.tensor_tensor(rstd[:, :], rstd[:, :], minus_half[:, :], ALU.pow).then_inc(rstd_ready, 1)
            pool.wait_ge(gate_ready, 1)
            pool.tensor_tensor(bo_rows[:, :], bo_rows[:, :], gate[:, 0:1].broadcast_to([P, D]), ALU.mult
                               ).then_inc(pool_step, 1)

            def mask_keys(t, b):
                pool.wait_ge(qk_ready, (t + 1) * 2)
                reused(pool, scored, t)
                pool.tensor_tensor(
                    k_masked[b][:, :, :, :],
                    k_t[b][:, :].rearrange("p (s a k) -> p s a k", s=PAIR, a=1).broadcast_to([P, PAIR, HG, S]),
                    head_mask[:, :].rearrange("p (a h c) -> p a h c", a=1, c=1).broadcast_to([P, PAIR, HG, S]),
                    ALU.mult).then_inc(k_masked_ready, 1)

            mask_keys(0, 0)
            pool.wait_ge(pool_step, 3)
            pool.tensor_tensor(x_biased[:, :, :], x_all[:, :, :],
                               bo_rows[:, :].rearrange("p (a d) -> p a d", a=1).broadcast_to([P, TILES, D]),
                               ALU.add).then_inc(xb_ready, 1)
            mask_keys(1, 1)

            def step(t, half, b):
                if has(t + 2):
                    mask_keys(t + 2, b)

            attention_sweep(pool, step)

            pool.wait_ge(ffn_stats, 2 * TILES)
            pool.tensor_scalar(rstd[:, :], mean_var[:, :, 1], 1.0 + EPS, EPS * EPS, ALU.mult, ALU.add
                               ).then_inc(pool_step, 1)
            pool.wait_ge(pool_step, 4)
            pool.tensor_tensor(rstd[:, :], rstd[:, :], minus_half[:, :], ALU.pow).then_inc(ffn_rstd, 1)

            def split(t, b):
                pool.wait_ge(copied, sims_job(t) + 1)
                if not (isinstance(t, int) and t < 2):
                    pool.wait_ge(copied, parts_job(t - 2) + 1)
                flat = sims[b][:, :, :]
                hi = parts[b][:, :, :, 0, :].rearrange("p h s k -> p (h s) k")
                lo = parts[b][:, :, :, 1, :].rearrange("p h s k -> p (h s) k")
                pool.tensor_tensor(lo, flat, hi, ALU.subtract).then_inc(parts_ready, 1)

            def add_input(t, half, b):
                pool.wait_ge(copied, (LAST_JOB if isinstance(t, int) and t == TILES - 1 else job(t + 1, "x")) + 1)
                if not (isinstance(t, int) and t < 2):
                    pool.wait_ge(stored[b], half * 16)
                pool.tensor_tensor(result[b][:, :], ffn_y[b][:, :], at(x2_all, t), ALU.add).then_inc(added, 1)

            def put_scores(t, n):
                h = ADDED[n]
                pool.wait_ge(base_ready, t * FH + (h + 1))
                pool.tensor_tensor(excess[h], excess[h], base[n][:, :], ALU.add).then_inc(put_together, 1)

            split(0, 0)

            def ffn_step(t, half, b, prev, next1, next2):
                if next1:
                    split(t + 1, 1 - b)
                for n in range(3):
                    put_scores(t, n)
                if prev:
                    add_input(t - 1, half - (1 - b), 1 - b)
                for n in range(3, len(ADDED)):
                    put_scores(t, n)

            ffn_sweep(pool, ffn_step)
            add_input(TILES - 1, (TILES - 1) // 2, (TILES - 1) % 2)

        @block.scalar
        def _(act):
            act.dma_start(x_all[:, :, :], x_view).then_inc(x_loaded, 16)
            act.dma_start(stage[:, :, :], wq_ffn.rearrange("d (n c) -> d n c", c=P)).then_inc(ffn_loaded, 16)
            act.dma_start(keys_sb[:, :, :, :], keys.rearrange("(g h) k s c -> (h k) g s c", g=FH * NK // P)).then_inc(ffn_loaded, 16)
            act.dma_start(down_sb[:, :, :], down.rearrange("(c p) d -> p c d", p=P)).then_inc(ffn_loaded, 16)
            act.dma_start(up_sb[:, :, :], up.rearrange("(c p) d -> p c d", p=P)).then_inc(ffn_loaded, 16)
            act.dma_start(norm_col[:, :], norm_w.rearrange("(d a) -> d a", a=1)).then_inc(ffn_loaded, 16)
            for n, g in enumerate((g_attn, g_ffn)):
                act.dma_start(gate_in[:, n:n + 1], g.rearrange("(a d) -> a d", a=1).broadcast_to([P, 1])
                              ).then_inc(x_loaded, 16)
            act.wait_ge(x_loaded, 48)
            act.activation(gate[:, :], gate_in[:, :], ACT.Tanh).then_inc(gate_ready, 1)
            act.wait_ge(w_transposed, 1)
            act.copy(weights_t[:, 0:3, :], ps_qk[:, 0:3, :]).then_inc(w_ready, 1)
            act.wait_ge(gate_ready, 1)
            act.activation(weights_t[:, 3, :], ps_qk[:, 3, :], ACT.Copy, scale=gate[:, 0:1]).then_inc(w_ready, 1)

            def copy_xc(t, b):
                act.wait_ge(xc_transposed, t + 1)
                reused(act, projected, t)
                reused(act, values_projected, t)
                act.copy(x_t[b][:, :], x_t_ps).then_inc(xc_ready, 1)
                act.copy(ctx_t[b][:, :, :, :],
                         ctx_t_ps.rearrange("p (s a k) -> p s a k", s=PAIR, a=1)
                         .broadcast_to([P, PAIR, 2, S])).then_inc(xc_ready, 1)

            def copy_qk(t, b):
                act.wait_ge(projected, t + 1)
                reused(act, scored, t)
                reused(act, k_masked_ready, t)
                act.activation(q_t[b][:, :], ps_qk[:, 0, :], ACT.Identity, bias=bias_cols[:, 0:1]).then_inc(qk_ready, 1)
                act.activation(k_t[b][:, :], ps_qk[:, 1, :], ACT.Identity, bias=bias_cols[:, 1:2]).then_inc(qk_ready, 1)

            def exponents(t, b):
                act.wait_ge(shift_done, t + 1)
                reused(act, probs_transposed, t)
                act.activation(probs[b][:, :], shifted[b][:, :], ACT.Exp, scale=SCALE).then_inc(exp_done, 1)

            def copy_mixed(t, b):
                act.wait_ge(mixed_transposed, t + 1)
                reused(act, attn_out, t)
                act.activation(mixed_t[b][:, :], mix_t_ps, ACT.Identity, bias=bias_cols[:, 2:3]
                               ).then_inc(mixed_t_ready, 1)

            def copy_probs(t, b):
                act.wait_ge(probs_transposed, t + 1)
                reused(act, mixed, t)
                act.copy(probs_t[b][:, :, :], probs_t_ps[:, :, :]).then_inc(probs_t_ready, 1)

            copy_xc(0, 0)
            copy_xc(1, 1)
            copy_qk(0, 0)
            copy_qk(1, 1)
            exponents(0, 0)

            def step(t, half, b):
                if has(t - 2):
                    if has(t + 2):
                        act.wait_ge(xc_transposed, t + 3)
                    copy_mixed(t - 2, b)
                if has(t + 2):
                    copy_xc(t + 2, b)
                    copy_qk(t + 2, b)
                if has(t + 1):
                    exponents(t + 1, 1 - b)
                if has(t):
                    copy_probs(t, b)

            attention_sweep(act, step)

            act.wait_ge(filled, KEYS_JOB + 1)
            act.copy(keys_t[:, :, :].rearrange("p n c -> p (n c)"), ring[0][:, 0:4 * P]).then_inc(copied, 1)
            for half in range(2):
                act.wait_ge(filled, WQ_JOB + half + 1)
                act.copy(wq_t[:, half * 8:half * 8 + 8, :].rearrange("p n c -> p (n c)"), ring[WQ_JOB + half]
                         ).then_inc(copied, 1)
            act.dma_start(stage[:, 0:E // P, :].rearrange("p n c -> p (n c)"), select_in).then_inc(sel_loaded, 16)
            act.wait_ge(ffn_loaded, 16 * 5)
            act.wait_ge(filled, DOWN_JOB + 1)
            act.activation(down_t[:, :, :].rearrange("p n c -> p (n c)"), ring[0], ACT.Copy, scale=norm_col[:, 0:1]
                           ).then_inc(copied, 1)
            act.wait_ge(filled, KEY_W_JOB + 1)
            act.activation(key_w[:, :], ring[1][:, 0:LISTS * NK], ACT.Copy, scale=norm_col[:, 0:1]).then_inc(copied, 1)
            act.wait_ge(sel_loaded, 16)
            act.copy(select[:, :], stage[:, 0:E // P, :].rearrange("p n c -> p (n c)")).then_inc(setup_ready, 1)

            def copy_turned(t, b, n):
                if not (isinstance(t, int) and t < 2):
                    act.wait_ge(filled, hidden_job(t - 2) + 1)
                act.copy(fn_t[b][:, :], ring[n][:, 0:P]).then_inc(copied, 1)

            def copy_sims(t, b, n):
                act.wait_ge(filled, sims_job(t) + 1)
                if not (isinstance(t, int) and t < 2):
                    act.wait_ge(least_ready, t - 1)
                    act.wait_ge(parts_ready, t - 1)
                    act.wait_ge(filled, parts_job(t - 2) + 1)
                act.copy(parts[b][:, :, :, 0, :].rearrange("p h s k -> p (h s) k").bitcast(F32R),
                         ring[n][:, 0:LISTS * NK].rearrange("p (n k) -> p n k", k=NK))
                act.copy(sims[b][:, :, :].rearrange("p n k -> p (n k)"), ring[n][:, 0:LISTS * NK]).then_inc(copied, 1)

            def gelu(t, b, n):
                act.wait_ge(filled, hidden_job(t) + 1)
                if not (isinstance(t, int) and t < 2):
                    act.wait_ge(y_ready, t - 1)
                act.activation(hidden[b][:, :], ring[n], ACT.Gelu).then_inc(copied, 1)

            def copy_parts(t, b, n):
                act.wait_ge(filled, parts_job(t) + 1)
                if not (isinstance(t, int) and t < 2):
                    act.wait_ge(filled, job(t - 2, "S7") + 1)
                act.copy(parts_t[b][:, :, :].rearrange("p n t -> p (n t)"), ring[n]).then_inc(copied, 1)

            def copy_excess(t, h, b):
                act.wait_ge(filled, job(t, f"S{h}") + 1)
                if h == ADDED[0]:
                    act.wait_ge(least_ready, t + 1)
                if not (isinstance(t, int) and t < 1):
                    act.wait_ge(head_summed, (t - 1) * FH + (h + 1))
                if h in ADDED:
                    act.activation(excess[h], ring[slot(t, f"S{h}")], ACT.Relu, bias=least_neg[b][:, h:h + 1]
                                   ).then_inc(copied, 1)
                else:
                    act.activation(excess[h], ring[slot(t, f"S{h}")], ACT.Relu).then_inc(copied, 1)

            for t in range(2):
                act.wait_ge(filled, turn_job(t) + 1)
                copy_turned(t, t, turn_job(t) % 3)
                copy_sims(t, t, sims_job(t) % 3)
            copy_parts(0, 0, parts_job(0) % 3)

            def ffn_step(t, half, b, prev, next1, next2):
                for h in range(3):
                    copy_excess(t, h, b)
                gelu(t, b, slot(t, "hid"))
                copy_excess(t, 3, b)
                if next1:
                    copy_parts(t + 1, 1 - b, slot(t, "split"))
                copy_excess(t, 4, b)
                copy_excess(t, 5, b)
                act.wait_ge(filled, job(t, "x") + 1)
                if prev:
                    if not (isinstance(t, int) and t < 3):
                        act.wait_ge(added, t - 2)
                    y = act.copy(ffn_y[1 - b][:, :], ring[slot(t, "x")][:, 512:512 + D])
                    if not next2:
                        y.then_inc(copied, 1)
                if next2:
                    copy_turned(t + 2, b, slot(t, "x"))
                copy_excess(t, 6, b)
                if next2:
                    copy_sims(t + 2, b, slot(t, "sim"))
                copy_excess(t, 7, b)

            ffn_sweep(act, ffn_step)
            act.wait_ge(filled, LAST_JOB + 1)
            act.wait_ge(added, TILES - 2)
            act.copy(ffn_y[(TILES - 1) % 2][:, :], ring[(LAST_JOB) % 3][:, 512:512 + D]).then_inc(copied, 1)

        @block.vector
        def _(dve):
            for b in range(2):
                dve.memset(v_blocks[b][:, :, :, 0:HD], 0.0).then_inc(ones_ready, 1)
            dve.wait_ge(x_loaded, 48)
            for t in range(TILES):
                dve.bn_stats(stats[:, t, :], x_all[:, t, :]).then_inc(stats_step, 1)
            dve.wait_ge(stats_step, TILES)
            for t in range(TILES):
                dve.bn_aggr(mean_var[:, t, :], stats[:, t, :]).then_inc(stats_step, 1)
            dve.wait_ge(stats_step, 2 * TILES)
            dve.wait_ge(rstd_ready, 1)

            def normalise(t, b):
                reused(dve, xc_transposed, t)
                mean = at(mean_var, t)[:, 0:1]
                scale = rstd[:, t:t + 1] if isinstance(t, int) else rstd[:, bass.ds(t, 1)]
                dve.tensor_scalar(xn[b][:, :], at(x_all, t), mean, scale, ALU.subtract, ALU.mult
                                  ).then_inc(xn_ready, 1)

            def block_values(t, b):
                dve.wait_ge(values_projected, t + 1)
                reused(dve, mixed, t)
                dve.tensor_tensor(
                    v_blocks[b][:, :, :, 0:HD],
                    ps_v[:, 0:PAIR, :].rearrange("p s (h e) -> p s h e", h=H),
                    value_mask[:, :].rearrange("p (a h c) -> p a h c", a=1, c=1).broadcast_to([P, PAIR, H, HD]),
                    ALU.mult).then_inc(v_ready, 1)

            def shift(t, b):
                dve.wait_ge(scored, t + 1)
                dve.tensor_reduce(row_max[:, :], scores_ps[:, :, :].rearrange("p g (h k) -> p g h k", h=HG), AX.X, ALU.max
                                  ).then_inc(max_ready, 1)
                dve.wait_ge(max_ready, t + 1)
                reused(dve, exp_done, t)
                dve.tensor_tensor(
                    shifted[b][:, :].rearrange("p (g h k) -> p g h k", g=G, h=HG),
                    scores_ps[:, :, :].rearrange("p g (h k) -> p g h k", h=HG),
                    row_max[:, :].rearrange("p (g h a) -> p g h a", g=G, a=1).broadcast_to([P, G, HG, S]),
                    ALU.subtract).then_inc(shift_done, 1)

            def divide(t, b):
                dve.wait_ge(mixed, t + 1)
                mix = mix_ps.rearrange("p (h e) -> p h e", h=H)
                dve.reciprocal(row_rec[:, :], mix[:, :, HD]).then_inc(rec_ready, 1)
                dve.wait_ge(rec_ready, t + 1)
                reused(dve, mixed_transposed, t)
                dve.tensor_tensor(mixed_sb[b][:, :].rearrange("p (h e) -> p h e", h=H), mix[:, :, 0:HD],
                                  row_rec[:, :].rearrange("p (h a) -> p h a", a=1).broadcast_to([P, H, HD]),
                                  ALU.mult).then_inc(mixed_ready, 1)

            def residual(t):
                dve.wait_ge(attn_out, t + 1)
                dve.tensor_tensor(at(x2_all, t), y_ps, at(x_biased, t), ALU.add).then_inc(x2_ready, 1)

            for t in range(3):
                normalise(t, t % 2)
            dve.wait_ge(ones_ready, 2 + 2 * PAIR)
            shift(0, 0)
            dve.wait_ge(xb_ready, 1)

            def step(t, half, b):
                if has(t - 2):
                    divide(t - 2, b)
                if has(t - 3):
                    dve.wait_ge(attn_out, t - 2)
                if has(t):
                    block_values(t, b)
                if has(t - 3):
                    residual(t - 3)
                if has(t + 1):
                    shift(t + 1, 1 - b)
                if has(t + 3):
                    normalise(t + 3, 1 - b)

            attention_sweep(dve, step)

            dve.wait_ge(ffn_loaded, 16 * 5)
            dve.tensor_scalar(up_sb[:, :, :], up_sb[:, :, :], gate[:, 1:2], None, ALU.mult).then_inc(setup_ready, 1)
            dve.wait_ge(x2_ready, TILES)
            for t in range(TILES):
                dve.bn_stats(stats[:, t, :], x2_all[:, t, :]).then_inc(ffn_stats, 1)
            dve.wait_ge(ffn_stats, TILES)
            for t in range(TILES):
                dve.bn_aggr(mean_var[:, t, :], stats[:, t, :]).then_inc(ffn_stats, 1)
            dve.wait_ge(ffn_stats, 2 * TILES)
            dve.wait_ge(ffn_rstd, 1)

            def normalise_ffn(t, b):
                if not (isinstance(t, int) and t < 2):
                    dve.wait_ge(copied, turn_job(t - 2) + 1)
                mean = at(mean_var, t)[:, 0:1]
                scale = rstd[:, t:t + 1] if isinstance(t, int) else rstd[:, bass.ds(t, 1)]
                dve.tensor_scalar(fn[b][:, :], at(x2_all, t), mean, scale, ALU.subtract, ALU.mult
                                  ).then_inc(fn_ready, 1)

            GROUPS = 10

            def group_done(t, n):
                dve.wait_ge(ranked, t * GROUPS + n)

            halves = (range(0, LISTS // 2), range(LISTS // 2, LISTS))

            def rank_first(t, b, half):
                for n in halves[half]:
                    last = dve.max(top[:, n, 0:8], sims[b][:, n, :])
                last.then_inc(ranked, 1)

            def rank_strike(t, b, half):
                for n in halves[half]:
                    last = dve.match_replace(struck[:, n, :], top[:, n, 0:8], sims[b][:, n, :], LOWEST)
                last.then_inc(ranked, 1)

            def rank_second(t, half):
                for n in halves[half]:
                    last = dve.max(top[:, n, 8:16], struck[:, n, :])
                last.then_inc(ranked, 1)

            def candidates(t):
                sides = top[:, :, :].rearrange("p (h s) k -> p h s k", s=SIDES)
                start, a = 0, 0
                while a < K:
                    width = REACH[a]
                    rows = REACH.count(width)
                    last = dve.tensor_tensor(
                        cand[:, :, start:start + rows * width].rearrange("p h (a b) -> p h a b", b=width),
                        sides[:, :, 0, a:a + rows].rearrange("p h (a b) -> p h a b", b=1).broadcast_to([P, FH, rows, width]),
                        sides[:, :, 1, 0:width].rearrange("p h (a b) -> p h a b", a=1).broadcast_to([P, FH, rows, width]),
                        ALU.add)
                    start += rows * width
                    a += rows
                last.then_inc(ranked, 1)

            def best_first():
                for h in range(FH):
                    last = dve.max(best[:, h, 0:8], cand[:, h, :])
                last.then_inc(ranked, 1)

            def best_strike():
                for h in range(FH):
                    last = dve.match_replace(cand_struck[:, h, :], best[:, h, 0:8], cand[:, h, :], LOWEST)
                last.then_inc(ranked, 1)

            def best_second():
                for h in range(FH):
                    last = dve.max(best[:, h, 8:16], cand_struck[:, h, :])
                last.then_inc(ranked, 1)

            def least_score(t, b):
                if not (isinstance(t, int) and t < 2):
                    dve.wait_ge(copied, job(t - 2, "S7") + 1)
                dve.tensor_scalar(least[b][:, :], best[:, :, K - 1], BELOW, 0.0, ALU.mult, ALU.max).then_inc(least_step, 1)
                dve.wait_ge(least_step, t + 1)
                dve.tensor_scalar(least_neg[b][:, :], least[b][:, :], -1.0, None, ALU.mult).then_inc(least_ready, 1)

            def head_base(t, h, b):
                dve.wait_ge(copied, job(t, f"S{h}") + 1)
                if h not in ADDED:
                    dve.scalar_tensor_tensor(out=excess[h], in0=excess[h], scalar=least[b][:, h:h + 1], in1=excess[h],
                                             op0=ALU.is_ge, op1=ALU.mult).then_inc(base_ready, 1)
                    return
                n = ADDED.index(h)
                if not (isinstance(t, int) and t < 1):
                    dve.wait_ge(put_together, (t - 1) * len(ADDED) + (n + 1))
                dve.tensor_scalar(base[n][:, :], excess[h], 0.0, least[b][:, h:h + 1], ALU.is_gt, ALU.mult
                                  ).then_inc(base_ready, 1)

            def weigh(t, b):
                dve.wait_ge(head_summed, (t + 1) * FH)
                dve.wait_ge(copied, hidden_job(t) + 1)
                if not (isinstance(t, int) and t < 1):
                    dve.wait_ge(filled, job(t, "x") + 1)
                dve.tensor_tensor(mix_y[:, :, :].rearrange("p n t -> p (n t)"), mix_w_ps, hidden[b][:, :], ALU.mult
                                  ).then_inc(y_ready, 1)

            def rank_wait(t, n):
                if n == 0:
                    dve.wait_ge(copied, sims_job(t) + 1)
                if n >= 2:
                    group_done(t, (1, 3, 4, 7, 8, 9)[n - 2])

            def rank(t, b, n):
                if n == 0:
                    rank_first(t, b, 0)
                if n == 1:
                    rank_first(t, b, 1)
                if n == 2:
                    rank_strike(t, b, 0)
                if n == 3:
                    rank_strike(t, b, 1)
                    rank_second(t, 0)
                if n == 4:
                    rank_second(t, 1)
                    group_done(t, 6)
                    candidates(t)
                if n == 5:
                    best_first()
                if n == 6:
                    best_strike()
                if n == 7:
                    best_second()
                    group_done(t, 10)
                    least_score(t, b)

            normalise_ffn(0, 0)
            normalise_ffn(1, 1)
            for n in range(8):
                rank_wait(0, n)
                rank(0, 0, n)

            def ffn_step(t, half, b, prev, next1, next2):
                if next2:
                    normalise_ffn(t + 2, b)
                for h in range(FH):
                    if h == 3 and prev:
                        weigh(t - 1, 1 - b)
                    if next1:
                        rank_wait(t + 1, h)
                    head_base(t, h, b)
                    if next1:
                        rank(t + 1, 1 - b, h)

            ffn_sweep(dve, ffn_step)
            weigh(TILES - 1, (TILES - 1) % 2)

        @block.tensor
        def _(pe):
            pe.wait_ge(w_loaded, 16 * N_W)
            for n in range(4):
                mm = pe.transpose(ps_qk[:, n, :], weights[:, n, :], ident[:, :])
            mm.then_inc(w_transposed, 1)

            def transpose_xc(t, half, b):
                pe.wait_ge(xn_ready, t + 1)
                pe.wait_ge(ctx_loaded[b], (half + 1) * 16)
                pe.transpose(x_t_ps, xn[b][:, :], ident[:, :])
                pe.transpose(ctx_t_ps, ctx_sb[b][:, :], ident[:, :]).then_inc(xc_transposed, 1)

            def project(t, b):
                pe.wait_ge(xc_ready, (t + 1) * 2)
                emptied(pe, qk_ready, t, 2)
                pe.matmul(ps_qk[:, 0, :], weights_t[:, 0, :], x_t[b][:, :], start=True, stop=True)
                pe.matmul(ps_qk[:, 1, :], weights_t[:, 1, :], ctx_t[b][:, :, 0, :], start=True, stop=True
                          ).then_inc(projected, 1)

            def project_values(t, b):
                emptied(pe, v_ready, t)
                for s in range(PAIR):
                    twice = ctx_t[b][:, s, :, :].rearrange("p a k -> p (a k)")
                    mm = pe.matmul(ps_v[:, s, :], twice, weights_t[:, 2, :], start=True, stop=True)
                mm.then_inc(values_projected, 1)

            def score(t, b):
                for g in range(G):
                    rows = slice(g * P // G, (g + 1) * P // G)
                    for s in range(PAIR):
                        mm = pe.matmul(scores_ps[s * S:(s + 1) * S, g, :], q_t[b][rows, s * S:(s + 1) * S],
                                       k_masked[b][rows, s, :, :], start=True, stop=True)
                mm.then_inc(scored, 1)

            def transpose_mixed(t, b):
                pe.wait_ge(mixed_ready, t + 1)
                pe.transpose(mix_t_ps, mixed_sb[b][:, :], ident[:, :]).then_inc(mixed_transposed, 1)

            def output(t, b):
                pe.wait_ge(mixed_t_ready, t + 1)
                pe.matmul(y_ps, mixed_t[b][:, :], weights_t[:, 3, :], start=True, stop=True).then_inc(attn_out, 1)

            def turn_and_mix(t, b, pairs):
                for p in pairs:
                    if has(t):
                        mm = pe.transpose(probs_t_ps[:, p, :], probs[b][:, p * P:(p + 1) * P], ident[:, :])
                        if p == HP - 1:
                            mm.then_inc(probs_transposed, 1)
                    if has(t - 1):
                        for s in range(PAIR):
                            mm = pe.matmul(mix_ps[s * S:(s + 1) * S, 2 * VW * p:2 * VW * (p + 1)],
                                           probs_t[1 - b][:, p, s * S:(s + 1) * S],
                                           v_blocks[1 - b][:, s, 2 * p:2 * p + 2, :], start=True, stop=True)
                        if p == HP - 1:
                            mm.then_inc(mixed, 1)

            pe.wait_ge(w_ready, 2)
            transpose_xc(0, 0, 0)
            pe.wait_ge(xc_ready, 2)
            transpose_xc(1, 0, 1)
            project(0, 0)
            project(1, 1)
            project_values(0, 0)
            pe.wait_ge(k_masked_ready, 1)
            score(0, 0)

            def step(t, half, b):
                if has(t + 1):
                    pe.wait_ge(k_masked_ready, t + 2)
                    pe.wait_ge(shift_done, t + 1)
                if has(t + 1) or has(t - 2):
                    pe.wait_ge(xc_ready, t * 2 + 4 if has(t + 1) else TILES * 2)
                if has(t - 3):
                    pe.wait_ge(mixed_t_ready, t - 2)
                if has(t + 2):
                    transpose_xc(t + 2, half + 1, b)
                if has(t + 1):
                    score(t + 1, 1 - b)
                if has(t - 2):
                    transpose_mixed(t - 2, b)
                if has(t):
                    pe.wait_ge(exp_done, t + 1)
                    emptied(pe, probs_t_ready, t)
                if has(t - 1):
                    pe.wait_ge(probs_t_ready, t)
                    pe.wait_ge(v_ready, t)
                    emptied(pe, mixed_ready, t - 1)
                turn_and_mix(t, b, range(0, HP // 2))
                if has(t + 2):
                    project(t + 2, b)
                if has(t - 3):
                    pe.wait_ge(x2_ready, t - 2)
                if has(t + 1):
                    project_values(t + 1, 1 - b)
                if has(t - 2):
                    output(t - 2, b)
                turn_and_mix(t, b, range(HP // 2, HP))

            attention_sweep(pe, step)

            pe.wait_ge(x2_ready, TILES)
            pe.wait_ge(ffn_loaded, 16 * 5)
            for g in range(2):
                for side in range(SIDES):
                    mm = pe.transpose(ring[0][:, (g * SIDES + side) * P:(g * SIDES + side + 1) * P], keys_sb[:, g, side, :],
                                      ident[:, :])
            mm.then_inc(filled, 1)
            for n in range(LISTS):
                mm = pe.transpose(ring[WQ_JOB + n // 8][:, n % 8 * P:(n % 8 + 1) * P], stage[:, n, :], ident[:, :])
                if n % 8 == 7:
                    mm.then_inc(filled, 1)
            pe.wait_ge(copied, KEYS_JOB + 1)
            for c in range(EC):
                mm = pe.transpose(ring[0][:, c * P:(c + 1) * P], down_sb[:, c, :], ident[:, :])
            mm.then_inc(filled, 1)
            pe.wait_ge(copied, WQ_JOB + 2)
            for h in range(FH):
                for side in range(SIDES):
                    n = h * SIDES + side
                    per = P // NK
                    mm = pe.matmul(ring[1][:, n * NK:(n + 1) * NK], wq_t[:, n, :],
                                   keys_t[:, h // per * SIDES + side, h % per * NK:(h % per + 1) * NK],
                                   start=True, stop=True)
            mm.then_inc(filled, 1)
            pe.wait_ge(setup_ready, 2)

            def ring_free(n):
                pe.wait_ge(copied, n - 2)

            def turn_input(t, b, n, last=True):
                pe.wait_ge(fn_ready, t + 1)
                pe.transpose(ring[n][:, 0:P], fn[b][:, :], ident[:, :]).then_inc(filled, 1)

            def similarities(t, b, n):
                pe.wait_ge(copied, turn_job(t) + 1)
                pe.matmul(ring[n][:, 0:LISTS * NK], fn_t[b][:, :], key_w[:, :], start=True, stop=True).then_inc(filled, 1)

            def experts(t, b, n):
                pe.wait_ge(copied, turn_job(t) + 1)
                for c in range(EC):
                    mm = pe.matmul(ring[n][:, c * P:(c + 1) * P], down_t[:, c, :], fn_t[b][:, :], start=True, stop=True)
                mm.then_inc(filled, 1)

            def turn_parts(t, b, n):
                pe.wait_ge(parts_ready, t + 1)
                for h in range(FH):
                    mm = pe.transpose(ring[n][:, h * P:(h + 1) * P], parts[b][:, h, :, :, :].rearrange("p s a k -> p (s a k)"),
                                      ident[:, :])
                mm.then_inc(filled, 1)

            def pair_scores(t, h, b):
                ring_free(job(t, f"S{h}"))
                if h == 0:
                    pe.wait_ge(copied, parts_job(t) + 1)
                for half in range(2):
                    cols = slice(half * 512, half * 512 + 512)
                    mm = pe.matmul(ring[slot(t, f"S{h}")][:, cols], parts_t[b][:, h, :], select[:, cols], start=True, stop=True)
                mm.then_inc(filled, 1)

            def sum_head(t, h):
                if h in ADDED:
                    pe.wait_ge(put_together, t * len(ADDED) + (ADDED.index(h) + 1))
                else:
                    pe.wait_ge(base_ready, t * FH + (h + 1))
                if h == 0 and not (isinstance(t, int) and t < 1):
                    pe.wait_ge(y_ready, t)
                for c in range(EC):
                    first = h == 0 and c % 4 == 0
                    mm = pe.matmul(mix_w_ps[:, c * P:(c + 1) * P], excess[h][:, c * P:(c + 1) * P], ident[:, :],
                                   is_transpose=True, start=first, stop=(h == FH - 1 and c % 4 == 3),
                                   skip_group_check=True)
                mm.then_inc(head_summed, 1)

            def ffn_out(t, n):
                pe.wait_ge(y_ready, t + 1)
                for c in range(EC):
                    mm = pe.matmul(ring[n][:, 512:512 + D], mix_y[:, c, :], up_sb[:, c, :], start=(c == 0), stop=(c == EC - 1))
                return mm

            for t in range(2):
                ring_free(turn_job(t))
                turn_input(t, t, turn_job(t) % 3)
                ring_free(sims_job(t))
                similarities(t, t, sims_job(t) % 3)
            ring_free(parts_job(0))
            turn_parts(0, 0, parts_job(0) % 3)

            def ffn_step(t, half, b, prev, next1, next2):
                for h in range(3):
                    pair_scores(t, h, b)
                    if prev:
                        sum_head(t - 1, 5 + h)
                ring_free(job(t, "hid"))
                experts(t, b, slot(t, "hid"))
                pair_scores(t, 3, b)
                if next1:
                    ring_free(job(t, "split"))
                    turn_parts(t + 1, 1 - b, slot(t, "split"))
                pair_scores(t, 4, b)
                pair_scores(t, 5, b)
                ring_free(job(t, "x"))
                if prev:
                    mm = ffn_out(t - 1, slot(t, "x"))
                    if not next2:
                        mm.then_inc(filled, 1)
                if next2:
                    turn_input(t + 2, b, slot(t, "x"))
                sum_head(t, 0)
                pair_scores(t, 6, b)
                sum_head(t, 1)
                if next2:
                    ring_free(job(t, "sim"))
                    similarities(t + 2, b, slot(t, "sim"))
                sum_head(t, 2)
                sum_head(t, 3)
                pair_scores(t, 7, b)
                sum_head(t, 4)

            ffn_sweep(pe, ffn_step)
            for h in range(5, FH):
                sum_head(TILES - 1, h)
            ring_free(LAST_JOB)
            ffn_out(TILES - 1, LAST_JOB % 3).then_inc(filled, 1)


def kernel(x, ctx_1024, g_xattn, g_ffn, L0_xattn_Wq, L0_xattn_bq, L0_xattn_Wk, L0_xattn_bk, L0_xattn_Wv,
           L0_xattn_bv, L0_xattn_Wo, L0_xattn_bo, L0_ffn_norm_w, L0_ffn_wq, L0_ffn_keys,
           L0_ffn_expert_down, L0_ffn_expert_up):
    import numpy as np
    import concourse.bacc as bacc
    from concourse.bass_utils import run_bass_kernel_spmd

    partition, expert = np.arange(P)[:, None], np.arange(E)
    side, key = partition // (2 * NK), partition % NK
    constants = {
        "ident": np.eye(P, dtype=np.float32),
        "head_mask": (partition % (P // G) // HD == np.arange(HG)).astype(np.float32),
        "value_mask": (partition // S == np.arange(H) % 2).astype(np.float32),
        "select": (np.where(side == 0, expert // NK, expert % NK) == key).astype(np.float32),
    }
    arrays = dict(x=x, ctx=ctx_1024, g_attn=g_xattn, g_ffn=g_ffn, wq=L0_xattn_Wq, bq=L0_xattn_bq, wk=L0_xattn_Wk,
                  bk=L0_xattn_bk, wv=L0_xattn_Wv, bv=L0_xattn_bv, wo=L0_xattn_Wo, bo=L0_xattn_bo, norm_w=L0_ffn_norm_w,
                  wq_ffn=L0_ffn_wq, keys=L0_ffn_keys, down=L0_ffn_expert_down, up=L0_ffn_expert_up, **constants)
    nc = bacc.Bacc("TRN2", target_bir_lowering=False, num_devices=1)
    feeds, args = {}, []
    for name, a in arrays.items():
        a = np.ascontiguousarray(a)
        feeds[f"in_{name}"] = a
        args.append(nc.dram_tensor(f"in_{name}", a.shape, mybir.dt.from_np(a.dtype), kind="ExternalInput").ap())
    args.append(nc.dram_tensor("out_x", x.shape, F32, kind="ExternalOutput").ap())
    flamingo_kernel(nc, *args)
    return run_bass_kernel_spmd(nc, [feeds], core_ids=[0]).results[0]["out_x"]
```

```python
from contextlib import ExitStack

import concourse.bass as bass
from concourse import mybir

ALU = mybir.AluOpType
ACT = mybir.ActivationFunctionType
AX = mybir.AxisListType
F32 = mybir.dt.float32
F32R = mybir.dt.float32r

P = 128
B, S = 32, 64
D = 128
T = B * S
TILES = T // P
PAIR = P // S
H = 16
HD = D // H
G = 2
HG = H // G
HP = H // 2
VW = HD + 1
FH = 8
K = 16
NK = 32
SIDES = 2
LISTS = FH * SIDES
E = NK * NK
EC = E // P
NEAR = 8
REACH = [min(K // (a + 1), NEAR) for a in range(NEAR)]
CAND = sum(REACH) + SIDES * NK
ADDED = (2, 4)
MASKED = tuple(h for h in range(FH) if h not in ADDED)
SUM_ORDER = (0, 1, 3, 2, 5, 4, 6, 7)
SUMS_LATER = 3
LOWEST = -3.0e38
BELOW = 1.0 - 2.0 ** -21
EPS = 1e-5
SCALE = float(HD) ** -0.5


def flamingo_kernel(nc, x, ctx_in, g_attn, g_ffn, wq, bq, wk, bk, wv, bv, wo, bo,
                    norm_w, wq_ffn, keys, down, up, ident_in, head_mask_in, value_mask_in, select_in, out):
    x_view = x.rearrange("(t two) s d -> (two s) t d", two=PAIR)
    ctx_view = ctx_in.rearrange("(t two) s d -> t (two s) d", two=PAIR)
    out_view = out.rearrange("(t two) s d -> (two s) t d", two=PAIR)

    with ExitStack() as stack:
        def sb(name, shape, dt=F32):
            return stack.enter_context(nc.sbuf_tensor(name, shape, dt))

        def ps(name, shape, dt=F32):
            return stack.enter_context(nc.psum_tensor(name, shape, dt))

        def sem(name):
            return stack.enter_context(nc.semaphore(name))

        ident = sb("ident", [P, P])
        head_mask = sb("head_mask", [P, HG])
        value_mask = sb("value_mask", [P, H])
        weights = sb("weights", [P, 4, D])
        weights_t = sb("weights_t", [P, 4, D])
        bias_rows = sb("bias_rows", [4, D])
        bias_cols = sb("bias_cols", [P, 4])
        gate_in = sb("gate_in", [P, 2])
        gate = sb("gate", [P, 2])
        bo_rows = sb("bo_rows", [P, D])
        minus_half = sb("minus_half", [P, TILES])

        x_all = sb("x_all", [P, TILES, D])
        x_biased = sb("x_biased", [P, TILES, D])
        x2_all = sb("x2_all", [P, TILES, D])
        stats = sb("stats", [P, TILES, 6])
        mean_var = sb("mean_var", [P, TILES, 2])
        rstd = sb("rstd", [P, TILES])
        ffn_mean_var = sb("ffn_mean_var", [P, TILES, 2])
        ffn_scale = sb("ffn_scale", [P, TILES])
        ffn_shift = sb("ffn_shift", [P, TILES])

        ctx_sb = [sb(f"ctx_sb{b}", [P, D]) for b in range(2)]
        xn = [sb(f"xn{b}", [P, D]) for b in range(2)]
        x_t = [sb(f"x_t{b}", [P, P]) for b in range(2)]
        ctx_t = [sb(f"ctx_t{b}", [P, PAIR, 2, S]) for b in range(2)]
        q_t = [sb(f"q_t{b}", [P, P]) for b in range(2)]
        k_t = [sb(f"k_t{b}", [P, P]) for b in range(2)]
        k_masked = [sb(f"k_masked{b}", [P, PAIR, HG, S]) for b in range(2)]
        v_blocks = [sb(f"v_blocks{b}", [P, PAIR, H, VW]) for b in range(2)]
        row_max = sb("row_max", [P, H])
        shifted = [sb(f"shifted{b}", [P, H * S]) for b in range(2)]
        probs = [sb(f"probs{b}", [P, H * S]) for b in range(2)]
        probs_t = [sb(f"probs_t{b}", [P, HP, P]) for b in range(2)]
        row_rec = sb("row_rec", [P, H])
        mixed_sb = [sb(f"mixed_sb{b}", [P, D]) for b in range(2)]
        mixed_t = [sb(f"mixed_t{b}", [P, P]) for b in range(2)]

        banks = ps("banks", [P, 8, 512])
        ps_turned, ps_qk, ps_v = (banks[:, n, :].rearrange("p (n c) -> p n c", n=4) for n in range(3))
        scores_ps = banks[:, 4:6, :]
        probs_t_ps = banks[:, 6:8, :].rearrange("p n (m c) -> p (n m) c", c=P)
        ring = [banks[:, n:n + 2, :].rearrange("p n c -> p (n c)") for n in (0, 4, 6)]
        mix_w_ps = banks[:, 2:4, :].rearrange("p n c -> p (n c)")
        x_t_ps, ctx_t_ps, mix_t_ps = (ps_turned[:, n, :] for n in range(3))
        mix_ps = banks[:, 3, 0:H * VW]
        y_ps = ps_v[:, PAIR, :]

        select = sb("select", [P, E], F32R)
        norm_col = sb("norm_col", [P, 1])
        stage = sb("stage", [P, LISTS, P])
        keys_sb = sb("keys_sb", [P, FH * NK // P, SIDES, P])
        down_sb = sb("down_sb", [P, EC, D])
        up_sb = sb("up_sb", [P, EC, D])
        keys_t = sb("keys_t", [P, 2 * SIDES, P])
        wq_t = sb("wq_t", [P, LISTS, P])
        key_w = sb("key_w", [P, LISTS * NK])
        down_t = sb("down_t", [P, EC, P])

        fn = [sb(f"fn{b}", [P, D]) for b in range(2)]
        fn_t = [sb(f"fn_t{b}", [P, P]) for b in range(2)]
        sims = [sb(f"sims{b}", [P, LISTS, NK]) for b in range(2)]
        parts = [sb(f"parts{b}", [P, FH, SIDES, 2, NK]) for b in range(2)]
        parts_t = [sb(f"parts_t{b}", [P, FH, P], F32R) for b in range(2)]
        struck = sb("struck", [P, LISTS, NK])
        top = sb("top", [P, LISTS, NEAR])
        cand = sb("cand", [P, FH, CAND])
        cand_struck = sb("cand_struck", [P, FH, CAND])
        best = sb("best", [P, FH, K])
        least = [sb(f"least{b}", [P, FH]) for b in range(2)]
        least_neg = [sb(f"least_neg{b}", [P, FH]) for b in range(2)]
        excess = [probs_t[n][:, :, :].rearrange("p n t -> p (n t)") for n in range(2)]
        excess += [buf[n][:, :] for buf in (shifted, probs) for n in range(2)]
        excess += [sb(f"excess{n}", [P, E])[:, :] for n in range(6, FH)]
        base = [sb(f"base{n}", [P, E]) for n in range(len(ADDED))]
        hidden = [sb(f"hidden{b}", [P, EC * P]) for b in range(2)]
        mix_y = sb("mix_y", [P, EC, P])
        ffn_y = sb("ffn_y", [P, D])
        result = sb("result", [P, D])

        ffn_loaded = sem("ffn_loaded")
        up_loaded = sem("up_loaded")
        filled = sem("filled")
        copied = sem("copied")
        setup_filled = sem("setup_filled")
        setup_copied = sem("setup_copied")
        key_w_ready = sem("key_w_ready")
        setup_ready = sem("setup_ready")
        ffn_stats = sem("ffn_stats")
        ffn_stats_ready = sem("ffn_stats_ready")
        ffn_rstd_step = sem("ffn_rstd_step")
        ffn_rstd = sem("ffn_rstd")
        fn_ready = sem("fn_ready")
        parts_ready = sem("parts_ready")
        ranked = sem("ranked")
        cand_ready = sem("cand_ready")
        least_step = sem("least_step")
        least_ready = sem("least_ready")
        signed = sem("signed")
        base_ready = sem("base_ready")
        masked = sem("masked")
        put_together = sem("put_together")
        head_summed = sem("head_summed")
        y_ready = sem("y_ready")
        added = sem("added")

        first_places = [banks[:, 1, :]] * 4 + [ring[1]]
        FIRST = len(first_places)
        BODY = ("hid", "S0", "S1", "S2", "split", "S3", "S4", "x", "S5", "S6", "sim", "S7")
        ABSENT = {TILES - 2: ("sim",), TILES - 1: ("sim", "split")}

        def job(t, kind):
            at = BODY.index(kind)
            if not isinstance(t, int):
                return t * len(BODY) + (FIRST + at)
            missing = sum(len(kinds) for body, kinds in ABSENT.items() if body < t)
            missing += sum(BODY.index(kind) < at for kind in ABSENT.get(t, ()))
            return FIRST + t * len(BODY) + at - missing

        def slot(t, kind):
            return (job(t, kind) if isinstance(t, int) else FIRST + BODY.index(kind)) % 3

        def summed(t, h):
            return t * FH + (SUM_ORDER.index(h) + 1)

        LAST_JOB = job(TILES, BODY[0])

        def turn_job(tile):
            return (0, 2)[tile] if isinstance(tile, int) and tile < 2 else job(tile - 2, "x")

        def sims_job(tile):
            return (1, 3)[tile] if isinstance(tile, int) and tile < 2 else job(tile - 2, "sim")

        def hidden_job(tile):
            return job(tile, "hid")

        def parts_job(tile):
            return 4 if isinstance(tile, int) and tile < 1 else job(tile - 1, "split")

        w_loaded = sem("w_loaded")
        consts_loaded = sem("consts_loaded")
        gates_loaded = sem("gates_loaded")
        x_loaded = [sem(f"x_loaded{n}") for n in range(2)]
        ctx_loaded = [sem(f"ctx_loaded{b}") for b in range(2)]
        w_transposed = sem("w_transposed")
        w_ready = sem("w_ready")
        gate_ready = sem("gate_ready")
        stats_step = sem("stats_step")
        stats_ready = sem("stats_ready")
        rstd_step = sem("rstd_step")
        rstd_ready = sem("rstd_ready")
        pool_step = sem("pool_step")
        xb_ready = sem("xb_ready")
        ones_ready = sem("ones_ready")
        xn_ready = sem("xn_ready")
        xc_transposed = sem("xc_transposed")
        xc_ready = sem("xc_ready")
        projected = sem("projected")
        values_projected = sem("values_projected")
        qk_ready = sem("qk_ready")
        k_masked_ready = sem("k_masked_ready")
        v_ready = sem("v_ready")
        scored = sem("scored")
        max_ready = sem("max_ready")
        shift_done = sem("shift_done")
        exp_done = sem("exp_done")
        probs_transposed = sem("probs_transposed")
        probs_t_ready = sem("probs_t_ready")
        mixed = sem("mixed")
        rec_ready = sem("rec_ready")
        mixed_ready = sem("mixed_ready")
        mixed_transposed = sem("mixed_transposed")
        mixed_t_ready = sem("mixed_t_ready")
        attn_out = sem("attn_out")
        x2_ready = sem("x2_ready")
        stored = sem("stored")

        N_W = 4 + 1
        N_CONSTS = 3 + 2 + 1

        GROUPS = (slice(0, 4), slice(4, TILES))
        FFN_GROUPS = (slice(0, TILES // 2), slice(TILES // 2, TILES))

        def attention_sweep(eng, step):
            for t in range(-1, 4):
                step(t, t // 2, t % 2)
            with eng.Fori(2, TILES // 2 - 2) as j:
                for b in range(2):
                    step(j * 2 + b, j, b)
            step(TILES - 4, TILES // 2 - 2, 0)

        def attention_tail(step, t):
            step(t, t // 2, t % 2)

        def has(t):
            return not isinstance(t, int) or 0 <= t < TILES

        def reused(eng, semaphore, t, per_tile=1):
            if not (isinstance(t, int) and t < 2):
                eng.wait_ge(semaphore, (t - 1) * per_tile)

        def emptied(eng, semaphore, t, per_tile=1):
            if not (isinstance(t, int) and t < 1):
                eng.wait_ge(semaphore, t * per_tile)

        def ffn_sweep(eng, step):
            for t in range(2):
                step(t, t, t > 0, True, True)
            with eng.Fori(1, TILES // 2 - 1) as j:
                for b in range(2):
                    step(j * 2 + b, b, True, True, True)
            for t in range(TILES - 2, TILES):
                step(t, t % 2, True, t + 1 < TILES, t + 2 < TILES)

        def at(buf, t):
            if isinstance(t, int):
                return buf[:, t, :]
            return buf[:, bass.ds(t, 1), :].rearrange("p a d -> p (a d)")

        STEPS = ("first", "struck", "best first", "best struck", "best second")

        TURNED = [keys_sb[:, n // SIDES, n % SIDES, :] for n in range(2 * SIDES)]
        TURNED += [stage[:, n, :] for n in range(LISTS)]
        TURNED += [down_sb[:, n, :] for n in range(EC)]
        SETUP_JOBS = len(TURNED) // 4
        WQ_JOB = 2 * SIDES // 4
        DOWN_JOB = WQ_JOB + LISTS // 4
        PRODUCT_BODIES = (2, 3)
        key_w_ps = ps_qk[:, 2:4, :].rearrange("p n c -> p (n c)")
        setup_banks = [banks[:, n, :] for n in (6, 7)]

        block = stack.enter_context(nc.Block())

        @block.sync
        def _(sp):
            sp.dma_start(ident[:, :], ident_in).then_inc(w_loaded, 16)
            for n, w in enumerate((wq, wk, wv, wo)):
                sp.dma_start(weights[:, n, :], w).then_inc(w_loaded, 16)
            for b in range(2):
                sp.dma_start(ctx_sb[b][:, :], ctx_view[b]).then_inc(ctx_loaded[b], 16)
            for n, v in enumerate((bq, bk, bv)):
                sp.dma_start(bias_cols[:, n:n + 1], v.rearrange("(d a) -> d a", a=1)).then_inc(consts_loaded, 16)
            sp.dma_start(head_mask[:, :], head_mask_in).then_inc(consts_loaded, 16)
            sp.dma_start(value_mask[:, :], value_mask_in).then_inc(consts_loaded, 16)
            sp.dma_start(bo_rows[:, :], bo.rearrange("(a d) -> a d", a=1).broadcast_to([P, D])).then_inc(consts_loaded, 16)

            sp.dma_start(keys_sb[:, :, :, :], keys.rearrange("(g h) k s c -> (h k) g s c", g=FH * NK // P)).then_inc(ffn_loaded, 16)
            sp.dma_start(stage[:, :, :], wq_ffn.rearrange("d (n c) -> d n c", c=P)).then_inc(ffn_loaded, 16)
            sp.dma_start(norm_col[:, :], norm_w.rearrange("(d a) -> d a", a=1)).then_inc(ffn_loaded, 16)
            sp.dma_start(down_sb[:, :, :], down.rearrange("(c p) d -> p c d", p=P)).then_inc(ffn_loaded, 16)
            sp.dma_start(up_sb[:, :, :], up.rearrange("(c p) d -> p c d", p=P)).then_inc(up_loaded, 16)
            sp.dma_start(mix_y[:, :, :].rearrange("p n c -> p (n c)"), select_in).then_inc(up_loaded, 16)

            with sp.Fori(1, TILES // 2) as j:
                for b in range(2):
                    sp.wait_ge(xc_transposed, j * 2 + b - 1)
                    sp.dma_start(ctx_sb[b][:, :], ctx_view[bass.ds(j * 2 + b, 1)].rearrange("a p d -> (a p) d")
                                 ).then_inc(ctx_loaded[b], 16)

            with sp.Fori(0, TILES) as t:
                sp.wait_ge(added, t + 1)
                sp.dma_start(out_view[:, bass.ds(t, 1), :].rearrange("p a d -> p (a d)"), result[:, :]).then_inc(stored, 16)
            sp.wait_ge(stored, 16 * TILES)

        @block.gpsimd
        def _(pool):
            pool.memset(minus_half[:, :], -0.5).then_inc(pool_step, 1)

            def reciprocal_std(n):
                tiles = GROUPS[n]
                pool.wait_ge(stats_ready, n + 1)
                pool.tensor_scalar(rstd[:, tiles], mean_var[:, tiles, 1], EPS, None, ALU.add).then_inc(rstd_step, 1)
                pool.wait_ge(rstd_step, n + 1)
                pool.tensor_tensor(rstd[:, tiles], rstd[:, tiles], minus_half[:, tiles], ALU.pow).then_inc(rstd_ready, 1)

            pool.wait_ge(pool_step, 1)
            reciprocal_std(0)
            pool.wait_ge(consts_loaded, 16 * N_CONSTS)
            for b in range(2):
                for s in range(PAIR):
                    pool.tensor_copy(v_blocks[b][:, s, :, HD], value_mask[:, :]).then_inc(ones_ready, 1)

            def add_bias(n):
                tiles = slice(n * TILES // 2, (n + 1) * TILES // 2)
                pool.tensor_tensor(x_biased[:, tiles, :], x_all[:, tiles, :],
                                   bo_rows[:, :].rearrange("p (a d) -> p a d", a=1).broadcast_to([P, TILES // 2, D]),
                                   ALU.add).then_inc(xb_ready, 1)

            def ffn_reciprocal(n):
                tiles, done = FFN_GROUPS[n], 3 * n
                pool.wait_ge(ffn_stats_ready, n + 1)
                pool.tensor_scalar(ffn_scale[:, tiles], ffn_mean_var[:, tiles, 1], 1.0 + EPS, EPS * EPS, ALU.mult, ALU.add
                                   ).then_inc(ffn_rstd_step, 1)
                pool.wait_ge(ffn_rstd_step, done + 1)
                pool.tensor_tensor(ffn_scale[:, tiles], ffn_scale[:, tiles], minus_half[:, tiles], ALU.pow
                                   ).then_inc(ffn_rstd_step, 1)
                pool.wait_ge(ffn_rstd_step, done + 2)
                pool.tensor_tensor(ffn_shift[:, tiles], ffn_mean_var[:, tiles, 0], ffn_scale[:, tiles], ALU.mult
                                   ).then_inc(ffn_rstd_step, 1)
                pool.wait_ge(ffn_rstd_step, done + 3)
                pool.tensor_scalar(ffn_shift[:, tiles], ffn_shift[:, tiles], -1.0, None, ALU.mult).then_inc(ffn_rstd, 1)

            def mask_keys(t, b):
                pool.wait_ge(qk_ready, (t + 1) * 2)
                reused(pool, scored, t)
                pool.tensor_tensor(
                    k_masked[b][:, :, :, :],
                    k_t[b][:, :].rearrange("p (s a k) -> p s a k", s=PAIR, a=1).broadcast_to([P, PAIR, HG, S]),
                    head_mask[:, :].rearrange("p (a h c) -> p a h c", a=1, c=1).broadcast_to([P, PAIR, HG, S]),
                    ALU.mult).then_inc(k_masked_ready, 1)

            mask_keys(0, 0)
            reciprocal_std(1)
            pool.wait_ge(gate_ready, 1)
            pool.tensor_tensor(bo_rows[:, :], bo_rows[:, :], gate[:, 0:1].broadcast_to([P, D]), ALU.mult
                               ).then_inc(pool_step, 1)
            pool.wait_ge(pool_step, 2)

            def step(t, half, b):
                if has(t + 2):
                    mask_keys(t + 2, b)
                if isinstance(t, int) and t in (0, 1):
                    add_bias(t)
                if isinstance(t, int) and t == TILES - 4:
                    ffn_reciprocal(0)

            attention_sweep(pool, step)
            attention_tail(step, TILES - 3)

            def split(t, b):
                pool.wait_ge(copied, sims_job(t) + 1)
                if not (isinstance(t, int) and t < 2):
                    pool.wait_ge(copied, parts_job(t - 2) + 1)
                flat = sims[b][:, :, :]
                hi = parts[b][:, :, :, 0, :].rearrange("p h s k -> p (h s) k")
                lo = parts[b][:, :, :, 1, :].rearrange("p h s k -> p (h s) k")
                pool.tensor_tensor(lo, flat, hi, ALU.subtract).then_inc(parts_ready, 1)

            def add_input(t):
                last = isinstance(t, int) and t == TILES - 1
                pool.wait_ge(copied, (LAST_JOB if last else job(t + 1, "x")) + 1)
                if not (isinstance(t, int) and t < 1):
                    pool.wait_ge(stored, t * 16)
                pool.tensor_tensor(result[:, :], ffn_y[:, :], at(x2_all, t), ALU.add).then_inc(added, 1)

            def candidates(t):
                pool.wait_ge(ranked, t * len(STEPS) + (STEPS.index("first") + 1))
                sides = top[:, :, :].rearrange("p (h s) k -> p h s k", s=SIDES)
                left = struck[:, :, :].rearrange("p (h s) k -> p h s k", s=SIDES)
                start = 0
                for width in sorted(set(REACH), reverse=True):
                    rows, a = REACH.count(width), REACH.index(width)
                    pool.tensor_tensor(
                        cand[:, :, start:start + rows * width].rearrange("p h (a b) -> p h a b", b=width),
                        sides[:, :, 0, a:a + rows].rearrange("p h (a b) -> p h a b", b=1).broadcast_to([P, FH, rows, width]),
                        sides[:, :, 1, 0:width].rearrange("p h (a b) -> p h a b", a=1).broadcast_to([P, FH, rows, width]),
                        ALU.add)
                    start += rows * width
                pool.wait_ge(ranked, t * len(STEPS) + (STEPS.index("struck") + 1))
                for side in range(SIDES):
                    last = pool.tensor_tensor(cand[:, :, start:start + NK], left[:, :, side, :],
                                              sides[:, :, 1 - side, 0:1].broadcast_to([P, FH, NK]), ALU.add)
                    start += NK
                last.then_inc(cand_ready, 1)

            def put_scores(t, n):
                h = ADDED[n]
                pool.wait_ge(base_ready, t * len(ADDED) + (n + 1))
                pool.tensor_tensor(excess[h], excess[h], base[n][:, :], ALU.add).then_inc(put_together, 1)

            split(0, 0)
            candidates(0)
            ffn_reciprocal(1)

            def ffn_step(t, b, prev, next1, next2):
                if next1:
                    split(t + 1, 1 - b)
                    candidates(t + 1)
                put_scores(t, 0)
                if prev:
                    add_input(t - 1)
                put_scores(t, 1)

            ffn_sweep(pool, ffn_step)
            add_input(TILES - 1)

        @block.scalar
        def _(act):
            act.dma_start(x_all[:, GROUPS[0], :], x_view[:, GROUPS[0], :]).then_inc(x_loaded[0], 16)
            for n, g in enumerate((g_attn, g_ffn)):
                act.dma_start(gate_in[:, n:n + 1], g.rearrange("(a d) -> a d", a=1).broadcast_to([P, 1])
                              ).then_inc(gates_loaded, 16)
            act.wait_ge(gates_loaded, 32)
            act.activation(gate[:, :], gate_in[:, :], ACT.Tanh).then_inc(gate_ready, 1)
            act.dma_start(x_all[:, GROUPS[1], :], x_view[:, GROUPS[1], :]).then_inc(x_loaded[1], 16)
            act.wait_ge(w_transposed, 1)
            act.copy(weights_t[:, 0:3, :], ps_qk[:, 0:3, :]).then_inc(w_ready, 1)
            act.wait_ge(gate_ready, 1)
            act.activation(weights_t[:, 3, :], ps_qk[:, 3, :], ACT.Copy, scale=gate[:, 0:1]).then_inc(w_ready, 1)

            def copy_xc(t, b):
                act.wait_ge(xc_transposed, t + 1)
                reused(act, projected, t)
                reused(act, values_projected, t)
                act.copy(x_t[b][:, :], x_t_ps).then_inc(xc_ready, 1)
                act.copy(ctx_t[b][:, :, :, :],
                         ctx_t_ps.rearrange("p (s a k) -> p s a k", s=PAIR, a=1)
                         .broadcast_to([P, PAIR, 2, S])).then_inc(xc_ready, 1)

            def copy_qk(t, b):
                act.wait_ge(projected, t + 1)
                reused(act, scored, t)
                reused(act, k_masked_ready, t)
                act.activation(q_t[b][:, :], ps_qk[:, 0, :], ACT.Identity, bias=bias_cols[:, 0:1]).then_inc(qk_ready, 1)
                act.activation(k_t[b][:, :], ps_qk[:, 1, :], ACT.Identity, bias=bias_cols[:, 1:2]).then_inc(qk_ready, 1)

            def exponents(t, b):
                act.wait_ge(shift_done, t + 1)
                reused(act, probs_transposed, t)
                act.activation(probs[b][:, :], shifted[b][:, :], ACT.Exp, scale=SCALE).then_inc(exp_done, 1)

            def copy_mixed(t, b):
                act.wait_ge(mixed_transposed, t + 1)
                reused(act, attn_out, t)
                act.activation(mixed_t[b][:, :], mix_t_ps, ACT.Identity, bias=bias_cols[:, 2:3]
                               ).then_inc(mixed_t_ready, 1)

            def copy_probs(t, b):
                act.wait_ge(probs_transposed, t + 1)
                reused(act, mixed, t)
                act.copy(probs_t[b][:, :, :], probs_t_ps[:, :, :]).then_inc(probs_t_ready, 1)

            copy_xc(0, 0)
            copy_xc(1, 1)
            act.wait_ge(consts_loaded, 16 * N_CONSTS)
            copy_qk(0, 0)

            def ffn_setup():
                act.wait_ge(ffn_loaded, 16 * 4)
                for n in range(SETUP_JOBS):
                    act.wait_ge(setup_filled, n + 1)
                    bank = setup_banks[n % 2]
                    if n < DOWN_JOB:
                        target = keys_t[:, :, :] if n < WQ_JOB else wq_t[:, 4 * (n - WQ_JOB):4 * (n - WQ_JOB) + 4, :]
                        act.copy(target.rearrange("p n c -> p (n c)"), bank).then_inc(setup_copied, 1)
                    else:
                        target = down_t[:, 4 * (n - DOWN_JOB):4 * (n - DOWN_JOB) + 4, :].rearrange("p n c -> p (n c)")
                        act.activation(target, bank, ACT.Copy, scale=norm_col[:, 0:1]).then_inc(setup_copied, 1)

            def step(t, half, b):
                if isinstance(t, int) and t in PRODUCT_BODIES:
                    act.wait_ge(projected, t + 3)
                    cols = slice(PRODUCT_BODIES.index(t) * 2 * P, (PRODUCT_BODIES.index(t) + 1) * 2 * P)
                    act.activation(key_w[:, cols], key_w_ps, ACT.Copy, scale=norm_col[:, 0:1]).then_inc(key_w_ready, 1)
                if has(t + 2):
                    copy_qk(t + 2, b)
                if has(t - 2):
                    copy_mixed(t - 2, b)
                if has(t + 3):
                    copy_xc(t + 3, 1 - b)
                if has(t + 1):
                    exponents(t + 1, 1 - b)
                if has(t):
                    copy_probs(t, b)
                if isinstance(t, int) and t == -1:
                    ffn_setup()
                if isinstance(t, int) and t == 3:
                    act.wait_ge(up_loaded, 32)
                    act.copy(select[:, :], mix_y[:, :, :].rearrange("p n c -> p (n c)")).then_inc(setup_ready, 1)

            def normalise_ffn(t, b):
                if not (isinstance(t, int) and t < 2):
                    act.wait_ge(filled, turn_job(t - 2) + 1)
                bias, scale = (v[:, t:t + 1] if isinstance(t, int) else v[:, bass.ds(t, 1)] for v in (ffn_shift, ffn_scale))
                act.activation(fn[b][:, :], at(x2_all, t), ACT.Identity, bias=bias, scale=scale).then_inc(fn_ready, 1)

            attention_sweep(act, step)
            act.wait_ge(ffn_rstd, 1)
            normalise_ffn(0, 0)
            normalise_ffn(1, 1)
            attention_tail(step, TILES - 3)

            def copy_turned(t, b, source):
                if not (isinstance(t, int) and t < 2):
                    act.wait_ge(filled, hidden_job(t - 2) + 1)
                act.copy(fn_t[b][:, :], source[:, 0:P]).then_inc(copied, 1)

            def copy_sims(t, b, source):
                act.wait_ge(filled, sims_job(t) + 1)
                if not (isinstance(t, int) and t < 2):
                    act.wait_ge(least_ready, t - 1)
                    act.wait_ge(parts_ready, t - 1)
                    act.wait_ge(filled, parts_job(t - 2) + 1)
                act.copy(parts[b][:, :, :, 0, :].rearrange("p h s k -> p (h s) k").bitcast(F32R),
                         source[:, 0:LISTS * NK].rearrange("p (n k) -> p n k", k=NK))
                act.copy(sims[b][:, :, :].rearrange("p n k -> p (n k)"), source[:, 0:LISTS * NK]).then_inc(copied, 1)

            def gelu(t, b, n):
                act.wait_ge(filled, hidden_job(t) + 1)
                if not (isinstance(t, int) and t < 2):
                    act.wait_ge(y_ready, t - 1)
                act.activation(hidden[b][:, :], ring[n], ACT.Gelu).then_inc(copied, 1)

            def copy_parts(t, b, source):
                act.wait_ge(filled, parts_job(t) + 1)
                if not (isinstance(t, int) and t < 2):
                    act.wait_ge(filled, job(t - 2, "S7") + 1)
                act.copy(parts_t[b][:, :, :].rearrange("p n t -> p (n t)"), source).then_inc(copied, 1)

            def copy_excess(t, h, b):
                act.wait_ge(filled, job(t, f"S{h}") + 1)
                if h == ADDED[0]:
                    act.wait_ge(least_ready, t + 1)
                if not (isinstance(t, int) and t < 1):
                    act.wait_ge(head_summed, summed(t - 1, h))
                if h in ADDED:
                    act.activation(excess[h], ring[slot(t, f"S{h}")], ACT.Relu, bias=least_neg[b][:, h:h + 1]
                                   ).then_inc(copied, 1)
                else:
                    act.activation(excess[h], ring[slot(t, f"S{h}")], ACT.Relu).then_inc(copied, 1)

            def sign_excess(t, n):
                act.wait_ge(copied, job(t, f"S{ADDED[n]}") + 1)
                if not (isinstance(t, int) and t < 1):
                    act.wait_ge(put_together, (t - 1) * len(ADDED) + (n + 1))
                act.activation(base[n][:, :], excess[ADDED[n]], ACT.Sign).then_inc(signed, 1)

            def scale_base(t, n, b):
                act.wait_ge(signed, t * len(ADDED) + (n + 1))
                act.activation(base[n][:, :], base[n][:, :], ACT.Copy, scale=least[b][:, ADDED[n]:ADDED[n] + 1]
                               ).then_inc(base_ready, 1)

            for t in range(2):
                act.wait_ge(filled, turn_job(t) + 1)
                copy_turned(t, t, first_places[turn_job(t)])
                attention_tail(step, TILES - 2 + 2 * t)
                copy_sims(t, t, first_places[sims_job(t)])
                attention_tail(step, TILES - 1 + 2 * t)
            copy_parts(0, 0, first_places[parts_job(0)])
            act.wait_ge(ffn_rstd, 2)

            def ffn_step(t, b, prev, next1, next2):
                if next2:
                    normalise_ffn(t + 2, b)
                gelu(t, b, slot(t, "hid"))
                copy_excess(t, 0, b)
                copy_excess(t, 1, b)
                copy_excess(t, 2, b)
                if next1:
                    copy_parts(t + 1, 1 - b, ring[slot(t, "split")])
                sign_excess(t, 0)
                copy_excess(t, 3, b)
                scale_base(t, 0, b)
                copy_excess(t, 4, b)
                act.wait_ge(filled, job(t, "x") + 1)
                if prev:
                    if not (isinstance(t, int) and t < 2):
                        act.wait_ge(added, t - 1)
                    y = act.copy(ffn_y[:, :], ring[slot(t, "x")][:, 512:512 + D])
                    if not next2:
                        y.then_inc(copied, 1)
                if next2:
                    copy_turned(t + 2, b, ring[slot(t, "x")])
                copy_excess(t, 5, b)
                sign_excess(t, 1)
                copy_excess(t, 6, b)
                scale_base(t, 1, b)
                if next2:
                    copy_sims(t + 2, b, ring[slot(t, "sim")])
                copy_excess(t, 7, b)

            ffn_sweep(act, ffn_step)
            act.wait_ge(filled, LAST_JOB + 1)
            act.wait_ge(added, TILES - 1)
            act.copy(ffn_y[:, :], ring[LAST_JOB % 3][:, 512:512 + D]).then_inc(copied, 1)

        @block.vector
        def _(dve):
            for b in range(2):
                dve.memset(v_blocks[b][:, :, :, 0:HD], 0.0).then_inc(ones_ready, 1)

            def statistics(n):
                tiles = range(TILES)[GROUPS[n]]
                dve.wait_ge(x_loaded[n], 16)
                for t in tiles:
                    dve.bn_stats(stats[:, t, :], x_all[:, t, :]).then_inc(stats_step, 1)
                dve.wait_ge(stats_step, tiles[-1] + 1)
                for t in tiles:
                    last = dve.bn_aggr(mean_var[:, t, :], stats[:, t, :])
                last.then_inc(stats_ready, 1)
                dve.wait_ge(stats_ready, n + 1)

            def normalise(t, b):
                reused(dve, xc_transposed, t)
                mean = at(mean_var, t)[:, 0:1]
                scale = rstd[:, t:t + 1] if isinstance(t, int) else rstd[:, bass.ds(t, 1)]
                dve.tensor_scalar(xn[b][:, :], at(x_all, t), mean, scale, ALU.subtract, ALU.mult
                                  ).then_inc(xn_ready, 1)

            def block_values(t, b):
                dve.wait_ge(values_projected, t + 1)
                reused(dve, mixed, t)
                dve.tensor_tensor(
                    v_blocks[b][:, :, :, 0:HD],
                    ps_v[:, 0:PAIR, :].rearrange("p s (h e) -> p s h e", h=H),
                    value_mask[:, :].rearrange("p (a h c) -> p a h c", a=1, c=1).broadcast_to([P, PAIR, H, HD]),
                    ALU.mult).then_inc(v_ready, 1)

            def shift(t, b):
                dve.wait_ge(scored, t + 1)
                dve.tensor_reduce(row_max[:, :], scores_ps[:, :, :].rearrange("p g (h k) -> p g h k", h=HG), AX.X, ALU.max
                                  ).then_inc(max_ready, 1)
                dve.wait_ge(max_ready, t + 1)
                reused(dve, exp_done, t)
                dve.tensor_tensor(
                    shifted[b][:, :].rearrange("p (g h k) -> p g h k", g=G, h=HG),
                    scores_ps[:, :, :].rearrange("p g (h k) -> p g h k", h=HG),
                    row_max[:, :].rearrange("p (g h a) -> p g h a", g=G, a=1).broadcast_to([P, G, HG, S]),
                    ALU.subtract).then_inc(shift_done, 1)

            def divide(t, b):
                dve.wait_ge(mixed, t + 1)
                mix = mix_ps.rearrange("p (h e) -> p h e", h=H)
                dve.reciprocal(row_rec[:, :], mix[:, :, HD]).then_inc(rec_ready, 1)
                dve.wait_ge(rec_ready, t + 1)
                reused(dve, mixed_transposed, t)
                dve.tensor_tensor(mixed_sb[b][:, :].rearrange("p (h e) -> p h e", h=H), mix[:, :, 0:HD],
                                  row_rec[:, :].rearrange("p (h a) -> p h a", a=1).broadcast_to([P, H, HD]),
                                  ALU.mult).then_inc(mixed_ready, 1)

            def residual(t):
                dve.wait_ge(attn_out, t + 1)
                dve.tensor_tensor(at(x2_all, t), y_ps, at(x_biased, t), ALU.add).then_inc(x2_ready, 1)

            def ffn_statistics(t):
                dve.wait_ge(x2_ready, t + 1)
                stats_t = stats[:, t, :] if isinstance(t, int) else stats[:, bass.ds(t, 1), :].rearrange("p a d -> p (a d)")
                dve.bn_stats(stats_t, at(x2_all, t)).then_inc(ffn_stats, 1)

            def ffn_aggregate(n):
                tiles = range(TILES)[FFN_GROUPS[n]]
                dve.wait_ge(ffn_stats, tiles[-1] + 1)
                for t in tiles:
                    last = dve.bn_aggr(ffn_mean_var[:, t, :], stats[:, t, :])
                last.then_inc(ffn_stats_ready, 1)

            statistics(0)
            dve.wait_ge(rstd_ready, 1)
            for t in range(3):
                normalise(t, t % 2)
            statistics(1)
            dve.wait_ge(ones_ready, 2 + 2 * PAIR)

            def step(t, half, b):
                if isinstance(t, int) and t == TILES - 4:
                    ffn_aggregate(0)
                if has(t - 2):
                    divide(t - 2, b)
                if has(t - 3):
                    dve.wait_ge(attn_out, t - 2)
                if has(t):
                    block_values(t, b)
                if has(t - 3):
                    if isinstance(t, int) and t == 3:
                        dve.wait_ge(xb_ready, 2)
                    residual(t - 3)
                if has(t + 1):
                    shift(t + 1, 1 - b)
                if has(t - 4):
                    ffn_statistics(t - 4)
                if isinstance(t, int) and t == 3:
                    dve.wait_ge(up_loaded, 32)
                    dve.tensor_scalar(up_sb[:, :, :], up_sb[:, :, :], gate[:, 1:2], None, ALU.mult).then_inc(setup_ready, 1)
                if isinstance(t, int) and t == 0:
                    dve.wait_ge(rstd_ready, 2)
                if has(t + 4):
                    normalise(t + 4, b)

            attention_sweep(dve, step)

            for t in range(TILES - 3, TILES):
                attention_tail(step, t)

            def step_done(t, name):
                dve.wait_ge(ranked, t * len(STEPS) + (STEPS.index(name) + 1))

            def rank_first(b, lists=range(LISTS)):
                for n in lists:
                    last = dve.max(top[:, n, :], sims[b][:, n, :])
                if n == LISTS - 1:
                    last.then_inc(ranked, 1)

            def rank_strike(b):
                for n in range(LISTS):
                    last = dve.match_replace(struck[:, n, :], top[:, n, :], sims[b][:, n, :], LOWEST)
                last.then_inc(ranked, 1)

            def best_first():
                for h in range(FH):
                    last = dve.max(best[:, h, 0:8], cand[:, h, :])
                last.then_inc(ranked, 1)

            def best_strike():
                for h in range(FH):
                    last = dve.match_replace(cand_struck[:, h, :], best[:, h, 0:8], cand[:, h, :], LOWEST)
                last.then_inc(ranked, 1)

            def best_second():
                for h in range(FH):
                    last = dve.max(best[:, h, 8:16], cand_struck[:, h, :])
                last.then_inc(ranked, 1)

            def least_score(t, b):
                step_done(t, "best second")
                if not (isinstance(t, int) and t < 2):
                    dve.wait_ge(copied, job(t - 2, "S7") + 1)
                dve.tensor_scalar(least[b][:, :], best[:, :, K - 1], BELOW, 0.0, ALU.mult, ALU.max).then_inc(least_step, 1)

            def negate_least(t, b):
                dve.wait_ge(least_step, t + 1)
                dve.tensor_scalar(least_neg[b][:, :], least[b][:, :], -1.0, None, ALU.mult).then_inc(least_ready, 1)

            def mask_scores(t, h, b, part=slice(0, E)):
                dve.wait_ge(copied, job(t, f"S{h}") + 1)
                scores = excess[h][:, part]
                mask = dve.scalar_tensor_tensor(out=scores, in0=scores, scalar=least[b][:, h:h + 1], in1=scores,
                                                op0=ALU.is_ge, op1=ALU.mult)
                if part.stop == E:
                    mask.then_inc(masked, 1)

            def mask_around(t, h, b, wait):
                mask_scores(t, h, b, slice(0, E // 2))
                wait()
                mask_scores(t, h, b, slice(E // 2, E))

            def weigh(t, b):
                dve.wait_ge(head_summed, (t + 1) * FH)
                dve.wait_ge(copied, hidden_job(t) + 1)
                if not (isinstance(t, int) and t < 1):
                    dve.wait_ge(filled, job(t, "x") + 1)
                dve.tensor_tensor(mix_y[:, :, :].rearrange("p n t -> p (n t)"), mix_w_ps, hidden[b][:, :], ALU.mult
                                  ).then_inc(y_ready, 1)

            dve.wait_ge(copied, sims_job(0) + 1)
            rank_first(0)
            attention_tail(step, TILES)
            step_done(0, "first")
            rank_strike(0)
            attention_tail(step, TILES + 1)
            attention_tail(step, TILES + 2)
            ffn_statistics(TILES - 1)
            ffn_aggregate(1)
            dve.wait_ge(cand_ready, 1)
            best_first()
            step_done(0, "best first")
            best_strike()
            step_done(0, "best struck")
            best_second()
            dve.wait_ge(copied, sims_job(1) + 1)

            def ffn_step(t, b, prev, next1, next2):
                half_lists = (range(LISTS // 2), range(LISTS // 2, LISTS)) if next1 else ((), ())

                def wait_candidates():
                    if next1:
                        dve.wait_ge(cand_ready, t + 2)

                def wait_best_first():
                    if next1:
                        step_done(t + 1, "best first")

                def wait_best_struck():
                    if next1:
                        step_done(t + 1, "best struck")
                    if next2:
                        dve.wait_ge(copied, sims_job(t + 2) + 1)

                if next1:
                    rank_first(1 - b, half_lists[0])
                least_score(t, b)
                if next1:
                    rank_first(1 - b, half_lists[1])
                negate_least(t, b)
                mask_scores(t, 0, b)
                if next1:
                    step_done(t + 1, "first")
                if prev:
                    weigh(t - 1, 1 - b)
                else:
                    mask_scores(t, 1, b)
                if next1:
                    rank_strike(1 - b)
                if prev:
                    mask_scores(t, 1, b)
                mask_around(t, 3, b, wait_candidates)
                if next1:
                    best_first()
                mask_around(t, 5, b, wait_best_first)
                if next1:
                    best_strike()
                mask_around(t, 6, b, wait_best_struck)
                if next1:
                    best_second()
                mask_scores(t, 7, b)

            ffn_sweep(dve, ffn_step)
            weigh(TILES - 1, (TILES - 1) % 2)

        @block.tensor
        def _(pe):
            pe.wait_ge(w_loaded, 16 * N_W)
            for n in range(4):
                mm = pe.transpose(ps_qk[:, n, :], weights[:, n, :], ident[:, :])
            mm.then_inc(w_transposed, 1)

            def transpose_xc(t, half, b):
                pe.wait_ge(xn_ready, t + 1)
                pe.wait_ge(ctx_loaded[b], (half + 1) * 16)
                pe.transpose(x_t_ps, xn[b][:, :], ident[:, :])
                pe.transpose(ctx_t_ps, ctx_sb[b][:, :], ident[:, :]).then_inc(xc_transposed, 1)

            def project(t, b):
                pe.wait_ge(xc_ready, (t + 1) * 2)
                emptied(pe, qk_ready, t, 2)
                pe.matmul(ps_qk[:, 0, :], weights_t[:, 0, :], x_t[b][:, :], start=True, stop=True)
                pe.matmul(ps_qk[:, 1, :], weights_t[:, 1, :], ctx_t[b][:, :, 0, :], start=True, stop=True
                          ).then_inc(projected, 1)

            def project_values(t, b):
                emptied(pe, v_ready, t)
                for s in range(PAIR):
                    twice = ctx_t[b][:, s, :, :].rearrange("p a k -> p (a k)")
                    mm = pe.matmul(ps_v[:, s, :], twice, weights_t[:, 2, :], start=True, stop=True)
                mm.then_inc(values_projected, 1)

            def score(t, b):
                for g in range(G):
                    rows = slice(g * P // G, (g + 1) * P // G)
                    for s in range(PAIR):
                        mm = pe.matmul(scores_ps[s * S:(s + 1) * S, g, :], q_t[b][rows, s * S:(s + 1) * S],
                                       k_masked[b][rows, s, :, :], start=True, stop=True)
                mm.then_inc(scored, 1)

            def transpose_mixed(t, b):
                pe.wait_ge(mixed_ready, t + 1)
                pe.transpose(mix_t_ps, mixed_sb[b][:, :], ident[:, :]).then_inc(mixed_transposed, 1)

            def output(t, b):
                pe.wait_ge(mixed_t_ready, t + 1)
                pe.matmul(y_ps, mixed_t[b][:, :], weights_t[:, 3, :], start=True, stop=True).then_inc(attn_out, 1)

            def turn_and_mix(t, b, pairs):
                for p in pairs:
                    if has(t):
                        mm = pe.transpose(probs_t_ps[:, p, :], probs[b][:, p * P:(p + 1) * P], ident[:, :])
                        if p == HP - 1:
                            mm.then_inc(probs_transposed, 1)
                    if has(t - 1):
                        for s in range(PAIR):
                            mm = pe.matmul(mix_ps[s * S:(s + 1) * S, 2 * VW * p:2 * VW * (p + 1)],
                                           probs_t[1 - b][:, p, s * S:(s + 1) * S],
                                           v_blocks[1 - b][:, s, 2 * p:2 * p + 2, :], start=True, stop=True)
                        if p == HP - 1:
                            mm.then_inc(mixed, 1)

            pe.wait_ge(w_ready, 2)
            transpose_xc(0, 0, 0)
            pe.wait_ge(xc_ready, 2)
            transpose_xc(1, 0, 1)
            project(0, 0)

            def ffn_setup():
                pe.wait_ge(ffn_loaded, 16 * 4)
                for n in range(SETUP_JOBS):
                    bank = setup_banks[n % 2]
                    if n >= 2:
                        pe.wait_ge(setup_copied, n - 1)
                    for c, source in enumerate(TURNED[4 * n:4 * n + 4]):
                        mm = pe.transpose(bank[:, c * P:(c + 1) * P], source, ident[:, :])
                    mm.then_inc(setup_filled, 1)

            def router_products(t, half):
                pe.wait_ge(setup_copied, SETUP_JOBS)
                emptied(pe, qk_ready, t, 2)
                lists = range(half * LISTS // 2, (half + 1) * LISTS // 2)
                for c, n in enumerate(lists):
                    h, side, per = n // SIDES, n % SIDES, P // NK
                    pe.matmul(key_w_ps[:, c * NK:(c + 1) * NK], wq_t[:, n, :],
                              keys_t[:, h // per * SIDES + side, h % per * NK:(h % per + 1) * NK], start=True, stop=True)

            def step(t, half, b):
                if has(t + 1):
                    pe.wait_ge(k_masked_ready, t + 2)
                    if not (isinstance(t, int) and t < 0):
                        pe.wait_ge(shift_done, t + 1)
                if isinstance(t, int) and t in PRODUCT_BODIES:
                    router_products(t + 2, PRODUCT_BODIES.index(t))
                if has(t + 2):
                    project(t + 2, b)
                if has(t + 1):
                    score(t + 1, 1 - b)
                if has(t - 2):
                    pe.wait_ge(xc_ready, t * 2 + 6 if has(t + 2) else TILES * 2)
                    transpose_mixed(t - 2, b)
                if isinstance(t, int) and t == 0:
                    pe.wait_ge(setup_copied, SETUP_JOBS)
                if has(t):
                    pe.wait_ge(exp_done, t + 1)
                    emptied(pe, probs_t_ready, t)
                if has(t - 1):
                    pe.wait_ge(probs_t_ready, t)
                    pe.wait_ge(v_ready, t)
                    emptied(pe, mixed_ready, t - 1)
                turn_and_mix(t, b, range(0, HP // 2))
                if has(t - 3):
                    pe.wait_ge(x2_ready, t - 2)
                if has(t + 1):
                    project_values(t + 1, 1 - b)
                if has(t - 2):
                    output(t - 2, b)
                if has(t + 3):
                    if not has(t - 2):
                        pe.wait_ge(xc_ready, (t + 3) * 2)
                    transpose_xc(t + 3, half + 1 + b, 1 - b)
                turn_and_mix(t, b, range(HP // 2, HP))
                if isinstance(t, int) and t == -1:
                    ffn_setup()

            attention_sweep(pe, step)

            attention_tail(step, TILES - 3)
            pe.wait_ge(qk_ready, TILES * 2)

            def ring_free(n):
                pe.wait_ge(copied, n - 2)

            def turn_input(t, b, target):
                pe.wait_ge(fn_ready, t + 1)
                pe.transpose(target[:, 0:P], fn[b][:, :], ident[:, :]).then_inc(filled, 1)

            def similarities(t, b, target):
                pe.wait_ge(copied, turn_job(t) + 1)
                pe.matmul(target[:, 0:LISTS * NK], fn_t[b][:, :], key_w[:, :], start=True, stop=True).then_inc(filled, 1)

            def experts(t, b, n):
                pe.wait_ge(copied, turn_job(t) + 1)
                for c in range(EC):
                    mm = pe.matmul(ring[n][:, c * P:(c + 1) * P], down_t[:, c, :], fn_t[b][:, :], start=True, stop=True)
                mm.then_inc(filled, 1)

            def turn_parts(t, b, target):
                pe.wait_ge(parts_ready, t + 1)
                for h in range(FH):
                    mm = pe.transpose(target[:, h * P:(h + 1) * P], parts[b][:, h, :, :, :].rearrange("p s a k -> p (s a k)"),
                                      ident[:, :])
                mm.then_inc(filled, 1)

            def pair_scores(t, h, b):
                ring_free(job(t, f"S{h}"))
                if h == 0:
                    pe.wait_ge(copied, parts_job(t) + 1)
                for half in range(2):
                    cols = slice(half * 512, half * 512 + 512)
                    mm = pe.matmul(ring[slot(t, f"S{h}")][:, cols], parts_t[b][:, h, :], select[:, cols], start=True, stop=True)
                mm.then_inc(filled, 1)

            def sum_head(t, h):
                if h in ADDED:
                    pe.wait_ge(put_together, t * len(ADDED) + (ADDED.index(h) + 1))
                else:
                    pe.wait_ge(masked, t * len(MASKED) + (MASKED.index(h) + 1))
                if h == SUM_ORDER[0] and not (isinstance(t, int) and t < 1):
                    pe.wait_ge(y_ready, t)
                for c in range(EC):
                    first = h == SUM_ORDER[0] and c % 4 == 0
                    mm = pe.matmul(mix_w_ps[:, c * P:(c + 1) * P], excess[h][:, c * P:(c + 1) * P], ident[:, :],
                                   is_transpose=True, start=first, stop=(h == SUM_ORDER[-1] and c % 4 == 3),
                                   skip_group_check=True)
                mm.then_inc(head_summed, 1)

            def ffn_out(t, n):
                pe.wait_ge(y_ready, t + 1)
                for c in range(EC):
                    mm = pe.matmul(ring[n][:, 512:512 + D], mix_y[:, c, :], up_sb[:, c, :], start=(c == 0), stop=(c == EC - 1))
                return mm

            for t in range(2):
                if t > 0:
                    pe.wait_ge(copied, turn_job(t))
                turn_input(t, t, first_places[turn_job(t)])
                attention_tail(step, TILES - 2 + 2 * t)
                pe.wait_ge(key_w_ready, len(PRODUCT_BODIES))
                similarities(t, t, first_places[sims_job(t)])
                attention_tail(step, TILES - 1 + 2 * t)
            turn_parts(0, 0, first_places[parts_job(0)])
            attention_tail(step, TILES + 2)
            pe.wait_ge(x2_ready, TILES)
            pe.wait_ge(setup_ready, 2)
            pe.wait_ge(probs_t_ready, TILES)

            def ffn_step(t, b, prev, next1, next2):
                ring_free(job(t, "hid"))
                experts(t, b, slot(t, "hid"))
                for h in range(SUMS_LATER):
                    pair_scores(t, h, b)
                    if prev:
                        sum_head(t - 1, SUM_ORDER[FH - SUMS_LATER + h])
                if next1:
                    ring_free(job(t, "split"))
                    turn_parts(t + 1, 1 - b, ring[slot(t, "split")])
                pair_scores(t, 3, b)
                pair_scores(t, 4, b)
                sum_head(t, SUM_ORDER[0])
                ring_free(job(t, "x"))
                if prev:
                    mm = ffn_out(t - 1, slot(t, "x"))
                    if not next2:
                        mm.then_inc(filled, 1)
                if next2:
                    turn_input(t + 2, b, ring[slot(t, "x")])
                pair_scores(t, 5, b)
                sum_head(t, SUM_ORDER[1])
                pair_scores(t, 6, b)
                sum_head(t, SUM_ORDER[2])
                if next2:
                    ring_free(job(t, "sim"))
                    similarities(t + 2, b, ring[slot(t, "sim")])
                sum_head(t, SUM_ORDER[3])
                pair_scores(t, 7, b)
                sum_head(t, SUM_ORDER[4])

            ffn_sweep(pe, ffn_step)
            for h in SUM_ORDER[FH - SUMS_LATER:]:
                sum_head(TILES - 1, h)
            ring_free(LAST_JOB)
            ffn_out(TILES - 1, LAST_JOB % 3).then_inc(filled, 1)


def kernel(x, ctx_1024, g_xattn, g_ffn, L0_xattn_Wq, L0_xattn_bq, L0_xattn_Wk, L0_xattn_bk, L0_xattn_Wv,
           L0_xattn_bv, L0_xattn_Wo, L0_xattn_bo, L0_ffn_norm_w, L0_ffn_wq, L0_ffn_keys,
           L0_ffn_expert_down, L0_ffn_expert_up):
    import numpy as np
    import concourse.bacc as bacc
    from concourse.bass_utils import run_bass_kernel_spmd

    partition, expert = np.arange(P)[:, None], np.arange(E)
    side, key = partition // (2 * NK), partition % NK
    constants = {
        "ident": np.eye(P, dtype=np.float32),
        "head_mask": (partition % (P // G) // HD == np.arange(HG)).astype(np.float32),
        "value_mask": (partition // S == np.arange(H) % 2).astype(np.float32),
        "select": (np.where(side == 0, expert // NK, expert % NK) == key).astype(np.float32),
    }
    arrays = dict(x=x, ctx=ctx_1024, g_attn=g_xattn, g_ffn=g_ffn, wq=L0_xattn_Wq, bq=L0_xattn_bq, wk=L0_xattn_Wk,
                  bk=L0_xattn_bk, wv=L0_xattn_Wv, bv=L0_xattn_bv, wo=L0_xattn_Wo, bo=L0_xattn_bo, norm_w=L0_ffn_norm_w,
                  wq_ffn=L0_ffn_wq, keys=L0_ffn_keys, down=L0_ffn_expert_down, up=L0_ffn_expert_up, **constants)
    nc = bacc.Bacc("TRN2", target_bir_lowering=False, num_devices=1)
    feeds, args = {}, []
    for name, a in arrays.items():
        a = np.ascontiguousarray(a)
        feeds[f"in_{name}"] = a
        args.append(nc.dram_tensor(f"in_{name}", a.shape, mybir.dt.from_np(a.dtype), kind="ExternalInput").ap())
    args.append(nc.dram_tensor("out_x", x.shape, F32, kind="ExternalOutput").ap())
    flamingo_kernel(nc, *args)
    return run_bass_kernel_spmd(nc, [feeds], core_ids=[0]).results[0]["out_x"]
```
